# Optimizing a Trainium2 kernel written in Bass

```python
import numpy as np
import jax
import jax.numpy as jnp

def _softmax(x, axis=-1):
    return jax.nn.softmax(x, axis=axis)

def _gelu(x):
    return jax.nn.gelu(x, approximate=True)

def _silu(x):
    return jax.nn.silu(x)

def _sigmoid(x):
    return jax.nn.sigmoid(x)

def _layernorm(x, axis=-1, eps=1e-05):
    m = jnp.mean(x, axis=axis, keepdims=True)
    v = jnp.var(x, axis=axis, keepdims=True)
    return (x - m) / jnp.sqrt(v + eps)

def _scatter_add(tgt, idx, src, axis=0):
    return tgt.at[idx].add(src)

def _segment_sum(src, seg, n):
    return jax.ops.segment_sum(src, seg, n)
kernel_name = 'mk_adj_preln_d2_adj_r2_e7982d'

def setup_inputs(seed: int=0):
    np.random.seed(seed)
    _w = jnp.asarray

    def _rec_inputs():
        import jax
        import jax.numpy as jnp
        _gk = jax.random.key(seed)
        x = -0.0001538 + 1 * jax.random.normal(jax.random.fold_in(_gk, 1), (128, 64, 384), jnp.float32)
        _a = jax.random.bernoulli(jax.random.fold_in(_gk, 2), 0.0625, (128, 64, 64))
        adj = _a.astype(jnp.int32)
        return (x, adj)
    x, adj = _rec_inputs()

    def _L0_gnn_setup():
        import jax, jax.numpy as jnp
        import numpy as np
        D = 384
        NEG = -1000000000.0
        key = jax.random.key(seed)
        ks = jax.random.split(key, 12)
        B, N = (8, 512)
        x = jax.random.normal(ks[0], (B, N, D), dtype=jnp.float32)
        section_mask_full = jax.random.randint(ks[1], (B, N, N), 0, 2, dtype=jnp.int32)
        sentence_mask_full = jax.random.randint(ks[2], (B, N, N), 0, 2, dtype=jnp.int32)
        s = 1.0 / np.sqrt(D)
        W1 = jax.random.normal(ks[3], (D, D), dtype=jnp.float32) * s
        b1 = jnp.zeros((D,), dtype=jnp.float32)
        W2 = jax.random.normal(ks[4], (D, D), dtype=jnp.float32) * s
        b2 = jnp.zeros((D,), dtype=jnp.float32)
        W3 = jax.random.normal(ks[5], (D, D), dtype=jnp.float32) * s
        b3 = jnp.zeros((D,), dtype=jnp.float32)
        W4 = jax.random.normal(ks[6], (D, D), dtype=jnp.float32) * s
        b4 = jnp.zeros((D,), dtype=jnp.float32)
        return {'x': x, 'section_mask_full': section_mask_full, 'sentence_mask_full': sentence_mask_full, 'W1': W1, 'b1': b1, 'W2': W2, 'b2': b2, 'W3': W3, 'b3': b3, 'W4': W4, 'b4': b4}
    _L0_gnn_all = _L0_gnn_setup()
    _L0_gnn_in = {k: v for k, v in _L0_gnn_all.items() if k in ('W1', 'b1', 'W2', 'b2', 'W3', 'b3', 'W4', 'b4')}
    del _L0_gnn_all

    def _L1_gnn_setup():
        import jax, jax.numpy as jnp
        import numpy as np
        B, L, H = (8, 128, 384)
        R = 128
        NUM_REL = 80
        NUM_BASE = NUM_REL // 2
        key = jax.random.key(seed)
        ks = jax.random.split(key, 12)
        s = 0.02
        E = jax.random.normal(ks[3], (NUM_REL, R), jnp.float32) * s
        E = E.at[0].set(0.0)
        return {'hidden_states': jax.random.normal(ks[0], (B, L, H), jnp.float32), 'heads': jax.random.randint(ks[1], (B, L, L), 0, 2), 'rels': jax.random.randint(ks[2], (B, L, L), 0, NUM_BASE), 'E': E, 'Wadj': jax.random.normal(ks[4], (H, H), jnp.float32) * s, 'badj': jnp.zeros((H,), jnp.float32), 'Wrev': jax.random.normal(ks[5], (H, H), jnp.float32) * s, 'brev': jnp.zeros((H,), jnp.float32), 'Wself': jax.random.normal(ks[6], (H, H), jnp.float32) * s, 'bself': jnp.zeros((H,), jnp.float32), 'Wr': jax.random.normal(ks[7], (H, R), jnp.float32) * s, 'br': jnp.zeros((H,), jnp.float32), 'Wrr': jax.random.normal(ks[8], (H, R), jnp.float32) * s, 'brr': jnp.zeros((H,), jnp.float32)}
    _L1_gnn_all = _L1_gnn_setup()
    _L1_gnn_in = {k: v for k, v in _L1_gnn_all.items() if k in ('E', 'Wadj', 'badj', 'Wrev', 'brev', 'Wself', 'bself', 'Wr', 'br', 'Wrr', 'brr')}
    del _L1_gnn_all
    return {'x': x, 'adj': adj, 'L0_gnn_W1': _L0_gnn_in['W1'], 'L0_gnn_b1': _L0_gnn_in['b1'], 'L0_gnn_W2': _L0_gnn_in['W2'], 'L0_gnn_b2': _L0_gnn_in['b2'], 'L0_gnn_W3': _L0_gnn_in['W3'], 'L0_gnn_b3': _L0_gnn_in['b3'], 'L0_gnn_W4': _L0_gnn_in['W4'], 'L0_gnn_b4': _L0_gnn_in['b4'], 'L1_gnn_E': _L1_gnn_in['E'], 'L1_gnn_Wadj': _L1_gnn_in['Wadj'], 'L1_gnn_badj': _L1_gnn_in['badj'], 'L1_gnn_Wrev': _L1_gnn_in['Wrev'], 'L1_gnn_brev': _L1_gnn_in['brev'], 'L1_gnn_Wself': _L1_gnn_in['Wself'], 'L1_gnn_bself': _L1_gnn_in['bself'], 'L1_gnn_Wr': _L1_gnn_in['Wr'], 'L1_gnn_br': _L1_gnn_in['br'], 'L1_gnn_Wrr': _L1_gnn_in['Wrr'], 'L1_gnn_brr': _L1_gnn_in['brr']}

def reference(x, adj, L0_gnn_W1, L0_gnn_b1, L0_gnn_W2, L0_gnn_b2, L0_gnn_W3, L0_gnn_b3, L0_gnn_W4, L0_gnn_b4, L1_gnn_E, L1_gnn_Wadj, L1_gnn_badj, L1_gnn_Wrev, L1_gnn_brev, L1_gnn_Wself, L1_gnn_bself, L1_gnn_Wr, L1_gnn_br, L1_gnn_Wrr, L1_gnn_brr):
    import jax
    import jax.numpy as jnp

    def _L0_gnn_ref(x, section_mask_full, sentence_mask_full, W1, b1, W2, b2, W3, b3, W4, b4):
        import jax, jax.numpy as jnp
        import numpy as np
        D = 384
        NEG = -1000000000.0
        sec = section_mask_full.astype(x.dtype)
        sen = sentence_mask_full.astype(x.dtype)
        mask0 = section_mask_full == 0
        mask1 = section_mask_full == 1
        q = x @ W1.T + b1
        k = x @ W2.T + b2
        att = jnp.einsum('bnd,bmd->bnm', q, k) / 28.0
        dia_att = jax.nn.softmax(jnp.where(mask0, NEG, att), axis=2)
        prior_att = jax.nn.softmax(jnp.where(mask0, NEG, 2.0 * sec + 4.0 * sen), axis=2)
        fusion_att = jax.nn.softmax(jnp.where(mask0, NEG, dia_att * prior_att), axis=2)
        g_x1 = jnp.einsum('bnm,bmd->bnd', fusion_att, x) @ W3.T + b3
        no_self_att = jax.nn.softmax(jnp.where(mask1, NEG, att), axis=2)
        g_x2 = jnp.einsum('bnm,bmd->bnd', no_self_att, g_x1) @ W4.T + b4
        return g_x1 + g_x2

    def _L1_gnn_ref(hidden_states, heads, rels, E, Wadj, badj, Wrev, brev, Wself, bself, Wr, br, Wrr, brr):
        import jax, jax.numpy as jnp
        import numpy as np
        B, L, H = (8, 128, 384)
        R = 128
        NUM_REL = 80
        NUM_BASE = NUM_REL // 2
        hs = hidden_states
        adj = heads.astype(hs.dtype)
        radj = jnp.swapaxes(adj, 1, 2)
        deg = adj.sum(-1)
        rdeg = radj.sum(-1)
        deg_c = jnp.where(deg > 0, deg, 1.0)
        rdeg_c = jnp.where(rdeg > 0, rdeg, 1.0)
        ctx = jnp.matmul(adj, hs @ Wadj.T + badj) / deg_c[..., None]
        ctx = ctx + jnp.matmul(radj, hs @ Wrev.T + brev) / rdeg_c[..., None]
        ctx = ctx + hs @ Wself.T + bself
        agg = jnp.einsum('bij,bijr->bir', adj, E[rels])
        rel = agg @ Wr.T + br * deg[..., None]
        rr = jnp.swapaxes(rels, 1, 2) + NUM_BASE
        rr = jnp.where(rr > NUM_BASE, rr, 0)
        ragg = jnp.einsum('bij,bijr->bir', radj, E[rr])
        rel = rel + ragg @ Wrr.T + brr * rdeg[..., None]
        return ctx + rel
    h = jnp.maximum(_layernorm(x, axis=-1), 0.0)
    x = x + _L0_gnn_ref(h, adj, adj, L0_gnn_W1, L0_gnn_b1, L0_gnn_W2, L0_gnn_b2, L0_gnn_W3, L0_gnn_b3, L0_gnn_W4, L0_gnn_b4)
    h = jnp.maximum(_layernorm(x, axis=-1), 0.0)
    x = x + _L1_gnn_ref(h, adj, adj, L1_gnn_E, L1_gnn_Wadj, L1_gnn_badj, L1_gnn_Wrev, L1_gnn_brev, L1_gnn_Wself, L1_gnn_bself, L1_gnn_Wr, L1_gnn_br, L1_gnn_Wrr, L1_gnn_brr)
    return x

_drawn_inputs = setup_inputs


def setup_inputs(seed=0):
    import zlib

    import numpy as np

    out = dict(_drawn_inputs(seed))
    spreads = {'L0_gnn_b1': (0.0, 0.8),
     'L0_gnn_b2': (0.0, 0.8),
     'L0_gnn_b3': (0.0, 0.1),
     'L0_gnn_b4': (0.0, 0.1),
     'L1_gnn_badj': (0.0, 0.1),
     'L1_gnn_brev': (0.0, 0.1),
     'L1_gnn_bself': (0.0, 0.1),
     'L1_gnn_br': (0.0, 0.1),
     'L1_gnn_brr': (0.0, 0.1)}
    factors = {'L0_gnn_W1': 5.242,
     'L0_gnn_W2': 5.11,
     'L1_gnn_E': 2.862,
     'L1_gnn_Wr': 4.793,
     'L1_gnn_Wrr': 4.059}
    for name, (base, spread) in spreads.items():
        noise = np.random.default_rng([zlib.crc32(name.encode()), seed]).standard_normal(out[name].shape)
        drawn = base * np.exp(spread * noise) if base else spread * noise
        out[name] = jnp.asarray(drawn.astype(out[name].dtype))
    for name, factor in factors.items():
        out[name] = (out[name] * factor).astype(out[name].dtype)
    return out
```

```python
from contextlib import ExitStack

import concourse.bass as bass
from concourse import mybir

F32 = mybir.dt.float32
F32R = mybir.dt.float32r
F16 = mybir.dt.float16
I32 = mybir.dt.int32
ALU = mybir.AluOpType
ACT = mybir.ActivationFunctionType
AX = mybir.AxisListType

P = 128
GRAPHS, N, D = 128, 64, 384
TILES = 4
W = TILES * P
ST = GRAPHS * N // W
C = D // P
R = 128
REL, REL_REV = 1, 41
EPS = 1e-5
H_SCALE = 64.0
F_SCALE = 1024.0
ATT_SCALE = 1.0 / (28.0 * H_SCALE * H_SCALE)
BIG = 1e9 / ATT_SCALE
LO = 32

J_YZ, J_HT, J_T, J_X1A, J_ADJT, J_X1B, J_T2, J_H2T, J_AGG, J_OUT, J_FT, J_AT, J_OUT3 = (
    0, 6, 9, 11, 13, 14, 16, 17, 20, 26, 35, 36, 37)


class Turn:

    def __init__(self, it, u):
        self.it, self.u = it, u

    def plus(self, n):
        return Turn(self.it, self.u + n)

    @property
    def par(self):
        return self.u % 2

    @property
    def index(self):
        return self.it * 2 + self.u

    def count(self, per, k):
        return self.it * (2 * per) + (self.u * per + k)

    def dma(self, per, k):
        return (self.it + self.u // 2) * (16 * per) + 16 * k


def wait(eng, sem, value):
    if isinstance(value, int) and value <= 0:
        return
    eng.wait_ge(sem, value)


def build(nc, x, adj, w0, b0, E, w1, b1, Wr, br, Wrr, brr, out):
    W1, W2, W3, W4 = w0
    Wadj, Wrev, Wself = w1

    x_v = x.rearrange("(s t h) n d -> s (h n) t d", t=TILES, h=2)
    out_v = out.rearrange("(s t h) n d -> s (h n) t d", t=TILES, h=2)
    adj_v = adj.rearrange("(s t h) i j -> s (h i) t j", t=TILES, h=2)

    with ExitStack() as ctx:
        def sb(name, shape, dt=F32):
            return ctx.enter_context(nc.sbuf_tensor(name, shape, dt))

        def sem(name):
            return ctx.enter_context(nc.semaphore(name))

        bank = [ctx.enter_context(nc.psum_tensor(f"bank{i}", [P, 512], F32)) for i in range(8)]

        def ps(job, n=512):
            return bank[job % 8][:, 0:n]

        names = ("G", "W34T", "W3T", "WadjT", "WrevT", "WselfT")
        w_hi = {k: sb(k + "_hi", [P, C, D], F32R) for k in names}
        w_lo = {k: sb(k + "_lo", [P, C, D], F32R) for k in names}
        W4T = sb("W4T", [P, C, D])
        WrTs = sb("WrTs", [P, 2, D])
        WrN = sb("WrN", [P, 2, C, R])
        relE = sb("relE", [P, 2])
        relL = sb("relL", [P, 2, 64])
        b1c = sb("b1c", [P, C])
        b3c = sb("b3c", [P, C])
        b3m = sb("b3m", [P, C, P])
        tb = sb("tb", [P, C])
        bias0 = sb("bias0", [P, D])
        b4bc = sb("b4bc", [P, D])
        rows = sb("rows", [64, D])
        rows_b = sb("rows_b", [64, D])
        rows_r = sb("rows_r", [64, D], F32R)
        rank = sb("rank", [64, D], F32R)
        id32 = sb("id32", [P, P])
        id16 = sb("id16", [P, P], F16)
        minus_half = sb("minus_half", [P, TILES])

        xin = sb("xin", [P, 2, TILES, D])
        x1 = sb("x1", [P, 2, TILES, D])
        h = sb("h", [P, TILES, D])
        h_hi = sb("h_hi", [P, 2, TILES, D], F16)
        h_lo = sb("h_lo", [P, 2, TILES, D], F16)
        h2_hi = sb("h2_hi", [P, TILES, D], F16)
        h2_lo = sb("h2_lo", [P, TILES, D], F16)
        hT = sb("hT", [P, C, W])
        hT_hi = sb("hT_hi", [P, C, W], F32R)
        hT_lo = sb("hT_lo", [P, C, W], F32R)
        tT = sb("tT", [P, C, W])
        yz_hi = sb("yz_hi", [P, C, TILES, 2 * P], F32R)
        yz_lo = sb("yz_lo", [P, C, TILES, 2 * P], F32R)
        st6 = sb("st6", [P, 2, TILES, 6])
        mv = sb("mv", [P, 2, TILES, 2])
        ve = sb("ve", [P, 2, TILES])
        rstd = sb("rstd", [P, 2, TILES])
        nmr = sb("nmr", [P, 2, TILES])
        spacer = sb("spacer", [P, 1])
        adj_i = sb("adj_i", [P, 2, TILES, N], I32)
        mask = sb("mask", [P, 2 * TILES, N])
        neg = sb("neg", [P, 2 * TILES, N])
        edges = sb("edges", [P, TILES, N])
        adj_b = sb("adj_b", [P, 2, TILES, 2 * P], F16)
        deg = sb("deg", [P, 2, TILES])
        ind = sb("ind", [P, 2, TILES])
        noedge = sb("noedge", [P, TILES])
        degc = sb("degc", [P, 2, TILES])
        rdeg = sb("rdeg", [P, 2, TILES])
        rdeg_h = sb("rdeg_h", [P, 2, 2, TILES])
        dcol = sb("dcol", [P, TILES, 4, 32], F16)
        drow = sb("drow", [64, 2, W], F32R)
        a = sb("a", [P, 2 * TILES, N])
        e = sb("e", [P, 2 * TILES, N])
        amax = sb("amax", [P, 2 * TILES])
        esum = sb("esum", [P, 2 * TILES])
        rsum = sb("rsum", [P, 2 * TILES])
        rsd = sb("rsd", [P, TILES])
        z = sb("z", [P, TILES, N])
        zx = sb("zx", [P, TILES, N])
        zm = sb("zm", [P, TILES, N])
        fsum = sb("fsum", [P, TILES])
        frec = sb("frec", [P, TILES])
        Fn = sb("Fn", [P, TILES, P])
        An = sb("An", [P, TILES, P])
        AT = sb("AT", [P, TILES, P])
        fa_hi = sb("fa_hi", [P, TILES, 2 * P], F16)
        fa_lo = sb("fa_lo", [P, TILES, 2 * P], F16)

        x1_flat = x1[:].rearrange("p a t d -> p (a t d)")

        def staged(flat, at=0):
            return flat[:, at:at + C * D].rearrange("p (c d) -> p c d", c=C)

        W1n, W2n = staged(x1_flat, 0), staged(x1_flat, C * D)
        W3n = staged(tT[:].rearrange("p c w -> p (c w)"))
        W4n = staged(hT[:].rearrange("p c w -> p (c w)"))

        x_in = [sem("x_in0"), sem("x_in1")]
        adj_in = [sem("adj_in0"), sem("adj_in1")]
        out_sent = [sem("out_sent0"), sem("out_sent1")]
        w_in = [sem(f"w_in{i}") for i in range(5)]
        c_in = sem("c_in")
        ident_ready, consts_ready, zeros_ready = sem("ident_ready"), sem("consts_ready"), sem("zeros_ready")
        prep_dve, prep_full, prep_hi, prep_lo = sem("prep_dve"), sem("prep_full"), sem("prep_hi"), sem("prep_lo")
        yz_full = sem("yz_full")
        hT_full = sem("hT_full")
        t_full = sem("t_full")
        x1_full = sem("x1_full")
        adjT_full = sem("adjT_full")
        drow_full = sem("drow_full")
        att_full = sem("att_full")
        h2T_full = sem("h2T_full")
        agg_full = sem("agg_full")
        out_full = sem("out_full")
        fT_full = sem("fT_full")
        aT_full = sem("aT_full")
        af_full = sem("af_full")
        s_yz_hi = sem("s_yz_hi")
        s_hT_hi = sem("s_hT_hi")
        s_tT = sem("s_tT")
        s_h2 = sem("s_h2")
        s_h2_hi = sem("s_h2_hi")
        s_adjT = sem("s_adjT")
        s_drow = sem("s_drow")
        s_h2T_hi = sem("s_h2T_hi")
        s_agg_hi = sem("s_agg_hi")
        s_exp = sem("s_exp")
        s_zexp = sem("s_zexp")
        s_h = sem("s_h")
        s_h_hi = sem("s_h_hi")
        s_fT_hi = sem("s_fT_hi")
        s_AT = sem("s_AT")
        s_af_hi = sem("s_af_hi")
        v_yz_lo = sem("v_yz_lo")
        v_hT_lo = sem("v_hT_lo")
        v_x1 = sem("v_x1")
        v_st = sem("v_st")
        v_mv = sem("v_mv")
        v_ve = sem("v_ve")
        v_nmr = sem("v_nmr")
        v_h2_lo = sem("v_h2_lo")
        v_h2T_lo = sem("v_h2T_lo")
        v_agg_lo = sem("v_agg_lo")
        v_adj = sem("v_adj")
        v_dcol = sem("v_dcol")
        v_a = sem("v_a")
        v_f = sem("v_f")
        v_An = sem("v_An")
        v_Fn = sem("v_Fn")
        v_st0 = sem("v_st0")
        v_mv0 = sem("v_mv0")
        v_ve0 = sem("v_ve0")
        v_nmr0 = sem("v_nmr0")
        v_fT_lo = sem("v_fT_lo")
        v_af_lo = sem("v_af_lo")
        v_out_step = sem("v_out_step")
        v_out = sem("v_out")
        g_xb = sem("g_xb")
        g_rstd = sem("g_rstd")
        g_rstd0 = sem("g_rstd0")
        g_h_lo = sem("g_h_lo")

        FULL = {"G": 1, "b1W2": 4, "W4T": 5, "W34T": 8, "bias": 11, "W3T": 12, "WrT": 15, "WrrT": 16,
                "WadjT": 17, "rows": 20, "WrevT": 21, "WselfT": 24}

        def prep_bank(name, c):
            return bank[(4 if name in ("W3T", "WrevT", "W4T") else 0) + c][:, 0:D]

        block = ctx.enter_context(nc.Block())

        def turns(eng, body, last):
            body(Turn(0, 0))
            body(Turn(0, 1))
            with eng.Fori(1, ST // 2 - 1) as it:
                body(Turn(it, 0))
                body(Turn(it, 1))
            body(Turn(ST // 2 - 1, 0))
            last(Turn(ST // 2 - 1, 1))

        def is_last(t, ahead):
            return isinstance(t.it, int) and t.index + ahead >= ST

        @block.sync
        def _(sp):
            def load(t):
                sp.dma_start(xin[:, t.par], x_v[t.index]).then_inc(x_in[t.par], 16)

            def load_adj(t):
                sp.dma_start(adj_i[:, t.par], adj_v[t.index]).then_inc(adj_in[t.par], 16)

            def natural(w):
                return w.rearrange("(c p) d -> p c d", p=P)

            load(Turn(0, 0))
            sp.dma_start(W1n, natural(W1)).then_inc(w_in[0], 16)
            sp.dma_start(W2n, natural(W2)).then_inc(w_in[0], 16)
            load_adj(Turn(0, 0))
            sp.dma_start(W4n, natural(W4)).then_inc(w_in[1], 16)
            sp.dma_start(W3n, natural(W3)).then_inc(w_in[1], 16)
            load(Turn(0, 1))
            load_adj(Turn(0, 1))
            sp.wait_ge(prep_full, 3)
            sp.dma_start(W1n, natural(Wadj)).then_inc(w_in[2], 16)
            sp.wait_ge(prep_full, 4)
            sp.dma_start(W2n, natural(Wrev)).then_inc(w_in[3], 16)
            sp.wait_ge(prep_full, FULL["W3T"] + 2)
            sp.dma_start(W3n, natural(Wself)).then_inc(w_in[4], 16)

            def turn(t):
                if not is_last(t, 2):
                    sp.wait_ge(g_xb, t.count(4, 4))
                    load(t.plus(2))
                    sp.wait_ge(v_adj, t.count(7, 7))
                    load_adj(t.plus(2))
                for i in range(TILES):
                    wait(sp, v_out, t.count(4, i + 1))
                    sp.dma_start(out_v[t.index][:, i], x1[:, t.par, i]).then_inc(out_sent[t.par], 16)

            turns(sp, turn, turn)
            for par in range(2):
                sp.wait_ge(out_sent[par], 16 * TILES * ST // 2)

        @block.gpsimd
        def _(pool):
            nc.gpsimd.memset(id32[:], 0.0).then_inc(zeros_ready, 1)
            nc.gpsimd.memset(id16[:], 0.0).then_inc(zeros_ready, 1)
            pool.wait_ge(zeros_ready, 2)
            for m in (id32, id16):
                nc.gpsimd.affine_select(out=m[:], in_=m[:], compare_op=ALU.not_equal, fill=1.0, base=0,
                                        pattern=[[-1, P]], channel_multiplier=1).then_inc(ident_ready, 1)
            nc.gpsimd.memset(minus_half[:], -0.5).then_inc(consts_ready, 1)
            nc.gpsimd.memset(relL[:], 0.0).then_inc(consts_ready, 1)
            nc.gpsimd.memset(rows_b[:], 0.0).then_inc(consts_ready, 1)
            for m in (adj_b, Fn, An):
                nc.gpsimd.memset(m[:], 0.0).then_inc(consts_ready, 1)
            nc.gpsimd.memset(dcol[:], 0.0).then_inc(consts_ready, 1)
            pool.wait_ge(consts_ready, 7)
            nc.gpsimd.memset(dcol[:, :, 0:2, 4], 1.0).then_inc(consts_ready, 1)

            def rstd_of(t, ready, signal, ln, part):
                pool.wait_ge(*ready)
                nc.gpsimd.tensor_tensor(rstd[:, ln, part], ve[:, ln, part], minus_half[:, part],
                                        ALU.pow).then_inc(signal, 1)

            def norm0(t):
                wait(pool, s_h_hi, t.count(4, 0))
                rstd_of(t, (v_ve0, t.count(1, 1)), g_rstd0, 0, slice(0, TILES))
                wait(pool, yz_full, t.count(6, -6))
                for i in range(TILES):
                    pool.wait_ge(s_h_hi, t.count(4, i + 1))
                    nc.gpsimd.tensor_tensor(h_lo[:, t.par, i], h[:, i], h_hi[:, t.par, i],
                                            ALU.subtract).then_inc(g_h_lo, 1)

            def add_bias(t):
                wait(pool, out_sent[t.par], t.dma(4, 0))
                pool.wait_ge(x_in[t.par], t.dma(1, 1))
                for i in range(TILES):
                    nc.gpsimd.tensor_tensor(x1[:, t.par, i], xin[:, t.par, i], bias0[:], ALU.add).then_inc(g_xb, 1)

            def turn(t):
                if not is_last(t, 1):
                    add_bias(t.plus(1))
                for i in range(TILES):
                    rstd_of(t, (v_ve, t.count(4, i + 1)), g_rstd, 1, slice(i, i + 1))
                if not is_last(t, 2):
                    norm0(t.plus(2))

            pool.wait_ge(consts_ready, 1)
            norm0(Turn(0, 0))
            pool.wait_ge(prep_full, FULL["WrevT"] + 2)
            pool.wait_ge(prep_dve, 9)
            add_bias(Turn(0, 0))
            norm0(Turn(0, 1))
            turns(pool, turn, turn)

        @block.scalar
        def _(act):
            def row(v):
                return v.rearrange("(a d) -> a d", a=1)

            for part in (0, LO):
                act.wait_ge(consts_ready, 3)
                for k, v in enumerate((br, brr, b1[0], b1[1], b1[2])):
                    act.dma_start(rows_b[part + k:part + k + 1, :], row(v)).then_inc(c_in, 16)
            act.dma_start(b1c[:], b0[0].rearrange("(c p) -> p c", p=P), allow_slow_non_contiguous=True).then_inc(c_in, 16)
            act.dma_start(b3c[:], b0[2].rearrange("(c p) -> p c", p=P), allow_slow_non_contiguous=True).then_inc(c_in, 16)
            act.dma_start(bias0[:], row(b0[2]).broadcast_to([P, D])).then_inc(c_in, 16)
            act.dma_start(b4bc[:], row(b0[3]).broadcast_to([P, D])).then_inc(c_in, 16)
            act.dma_start(relE[:, 0:1], E[REL:REL + 1, :].rearrange("a r -> r a"), allow_slow_non_contiguous=True).then_inc(c_in, 16)
            act.dma_start(relE[:, 1:2], E[REL_REV:REL_REV + 1, :].rearrange("a r -> r a"), allow_slow_non_contiguous=True).then_inc(c_in, 16)
            act.dma_start(WrN[:, 0], Wr.rearrange("(c p) r -> p c r", p=P)).then_inc(c_in, 16)
            act.dma_start(WrN[:, 1], Wrr.rearrange("(c p) r -> p c r", p=P)).then_inc(c_in, 16)

            def norm0(t):
                act.wait_ge(x_in[t.par], t.dma(1, 1))
                act.wait_ge(v_nmr0, t.count(1, 1))
                wait(act, v_h2_lo, t.count(4, -4))
                for i in range(TILES):
                    nc.scalar.activation(h[:, i], xin[:, t.par, i], ACT.Relu, bias=nmr[:, 0, i:i + 1],
                                         scale=rstd[:, 0, i:i + 1]).then_inc(s_h, 1)
                for i in range(TILES):
                    act.wait_ge(s_h, t.count(4, i + 1))
                    nc.scalar.activation(h_hi[:, t.par, i], h[:, i], ACT.Copy).then_inc(s_h_hi, 1)

            def copy_hT(t):
                for c in range(C):
                    act.wait_ge(hT_full, t.count(3, c + 1))
                    nc.scalar.activation(hT[:, c], ps(J_HT + c), ACT.Copy)
                    nc.scalar.activation(hT_hi[:, c], ps(J_HT + c), ACT.Copy).then_inc(s_hT_hi, 1)

            def copy_tT(t, c):
                act.wait_ge(t_full, t.count(3, c + 1))
                nc.scalar.activation(tT[:, c], ps(J_T + c if c < 2 else J_T2), ACT.Identity,
                                     bias=tb[:, c:c + 1]).then_inc(s_tT, 1)

            def copy_adjT(t):
                act.wait_ge(v_dcol, t.count(11, 1))
                nc.scalar.activation(adj_b[:, t.par, :, 0:P],
                                     bank[J_ADJT % 8][:].bitcast(F16)[:, 0:W].rearrange("p (t i) -> p t i", t=TILES),
                                     ACT.Copy).then_inc(s_adjT, 1)

            def copy_drow(t):
                act.wait_ge(drow_full, t.count(1, 1))
                nc.scalar.activation(drow[:, t.par], bank[J_ADJT % 8][0:64].bitcast(F16)[:, W:2 * W],
                                     ACT.Copy).then_inc(s_drow, 1)

            def norm1(t, i):
                act.wait_ge(v_nmr, t.count(4, i + 1))
                if i == 0 and not is_last(t, 1):
                    wait(act, g_h_lo, t.plus(1).count(4, 4))
                nc.scalar.activation(h[:, i], x1[:, t.par, i], ACT.Relu, bias=nmr[:, 1, i:i + 1],
                                     scale=rstd[:, 1, i:i + 1]).then_inc(s_h2, 1)
                act.wait_ge(s_h2, t.count(4, i + 1))
                nc.scalar.activation(h2_hi[:, i], h[:, i], ACT.Copy).then_inc(s_h2_hi, 1)

            def exps(t):
                act.wait_ge(v_a, t.count(4, 4))
                nc.scalar.activation(e[:], a[:], ACT.Exp, scale=ATT_SCALE).then_inc(s_exp, 1)
                act.wait_ge(v_f, t.count(8, 5))
                nc.scalar.activation(zx[:], z[:], ACT.Exp).then_inc(s_zexp, 1)

            def copy_fT(t):
                act.wait_ge(fT_full, t.count(1, 1))
                nc.scalar.activation(fa_hi[:, :, 0:P], ps(J_FT).rearrange("p (t i) -> p t i", t=TILES),
                                     ACT.Copy, scale=F_SCALE).then_inc(s_fT_hi, 1)
                act.wait_ge(aT_full, t.count(1, 1))
                nc.scalar.activation(AT[:], ps(J_AT).rearrange("p (t i) -> p t i", t=TILES),
                                     ACT.Copy).then_inc(s_AT, 1)

            def copy_af(t):
                act.wait_ge(af_full, t.count(1, 1))
                nc.scalar.activation(fa_hi[:, :, P:2 * P], ps(J_AT).rearrange("p (t i) -> p t i", t=TILES),
                                     ACT.Copy, scale=F_SCALE).then_inc(s_af_hi, 1)

            def pair(job):
                return bank[job % 8][:].rearrange("p (t i) -> p t i", t=2)

            def turn(t):
                n = t.plus(1)
                more = not is_last(t, 1)
                for k in range(2 * C):
                    act.wait_ge(yz_full, t.count(6, k + 1))
                    nc.scalar.activation(yz_hi[:, k // 2, 2 * (k % 2):2 * (k % 2) + 2], pair(J_YZ + k), ACT.Copy,
                                         scale=1.0 / (H_SCALE * F_SCALE)).then_inc(s_yz_hi, 1)
                if more:
                    copy_hT(n)
                    copy_tT(n, 0)
                    copy_tT(n, 1)
                norm1(t, 0)
                norm1(t, 1)
                if more:
                    copy_adjT(n)
                norm1(t, 2)
                if more:
                    copy_tT(n, 2)
                norm1(t, 3)
                if more:
                    copy_drow(n)
                for c in range(C):
                    act.wait_ge(h2T_full, t.count(3, c + 1))
                    nc.scalar.activation(hT_hi[:, c], ps(J_H2T + c), ACT.Copy).then_inc(s_h2T_hi, 1)
                for k in range(2 * C):
                    act.wait_ge(agg_full, t.count(6, k + 1))
                    nc.scalar.activation(yz_hi[:, k // 2, 2 * (k % 2):2 * (k % 2) + 2], pair(J_AGG + k),
                                         ACT.Copy).then_inc(s_agg_hi, 1)
                if more:
                    exps(n)
                if not is_last(t, 2):
                    norm0(t.plus(2))
                if more:
                    copy_fT(n)
                    copy_af(n)

            norm0(Turn(0, 0))
            for name, c in [(k, c) for k in names for c in range(C)]:
                act.wait_ge(prep_full, FULL[name] + c)
                nc.scalar.activation(w_hi[name][:, c], prep_bank(name, c),
                                     ACT.Copy).then_inc(prep_hi, 1)
            first = Turn(0, 0)
            copy_hT(first)
            for c in range(C):
                copy_tT(first, c)
            copy_adjT(first)
            copy_drow(first)
            exps(first)
            norm0(Turn(0, 1))
            copy_fT(first)
            copy_af(first)
            turns(act, turn, turn)

        @block.vector
        def _(dve):
            def norm0_stats(t):
                dve.wait_ge(x_in[t.par], t.dma(1, 1))
                for i in range(TILES):
                    nc.vector.bn_stats(st6[:, 0, i], xin[:, t.par, i]).then_inc(v_st0, 1)
                dve.wait_ge(v_st0, t.count(4, 4))
                nc.vector.memset(spacer[:], 0.0)
                for i in range(TILES):
                    nc.vector.bn_aggr(mv[:, 0, i], st6[:, 0, i]).then_inc(v_mv0, 1)
                dve.wait_ge(v_mv0, t.count(4, 4))
                wait(dve, g_rstd0, t.count(1, 0))
                nc.vector.tensor_scalar(ve[:, 0], mv[:, 0, :, 1], EPS, H_SCALE ** -2, ALU.add,
                                        ALU.mult).then_inc(v_ve0, 1)

            def norm0_shift(t):
                dve.wait_ge(g_rstd0, t.count(1, 1))
                wait(dve, s_h, t.count(4, 0))
                nc.vector.scalar_tensor_tensor(out=nmr[:, 0], in0=mv[:, 0, :, 0], scalar=-1.0, in1=rstd[:, 0],
                                               op0=ALU.mult, op1=ALU.mult).then_inc(v_nmr0, 1)

            def split_hT(t):
                for c in range(C):
                    dve.wait_ge(s_hT_hi, t.count(3, c + 1))
                    nc.vector.tensor_tensor(hT_lo[:, c], ps(J_HT + c), hT_hi[:, c].bitcast(F32),
                                            ALU.subtract).then_inc(v_hT_lo, 1)

            def masks(t):
                adj_f = mask[:, 0:TILES]
                dve.wait_ge(adj_in[t.par], t.dma(1, 1))
                nc.vector.tensor_copy(adj_f, adj_i[:, t.par]).then_inc(v_adj, 1)
                dve.wait_ge(v_adj, t.count(7, 1))
                nc.vector.tensor_scalar(mask[:, TILES:], adj_f, -1.0, 1.0, ALU.mult, ALU.add).then_inc(v_adj, 1)
                nc.vector.tensor_scalar(neg[:, 0:TILES], adj_f, -1.0, BIG, ALU.add, ALU.mult).then_inc(v_adj, 1)
                nc.vector.tensor_scalar(neg[:, TILES:], adj_f, -BIG, None, ALU.mult).then_inc(v_adj, 1)
                nc.vector.tensor_reduce(deg[:, 0], adj_f, AX.X, ALU.add).then_inc(v_adj, 1)
                if isinstance(t.it, int) and t.index == 0:
                    dve.wait_ge(consts_ready, 8)
                for g in range(2):
                    r = slice(g * N, (g + 1) * N)
                    nc.vector.tensor_copy(adj_b[r, t.par, :, P + g * N:P + (g + 1) * N],
                                          mask[r, 0:TILES]).then_inc(v_adj, 1)

            def degrees(t):
                def done(k):
                    dve.wait_ge(v_dcol, t.count(11, k))

                adjT = bank[J_ADJT % 8][:].bitcast(F16)[:, 0:W].rearrange("p (t i) -> p t i", t=TILES)
                dve.wait_ge(adjT_full, t.count(1, 1))
                dve.wait_ge(v_adj, t.count(7, 7))
                nc.vector.tensor_reduce(deg[:, 1], adjT, AX.X, ALU.add).then_inc(v_dcol, 1)
                done(1)
                nc.vector.tensor_scalar(ind[:], deg[:], 1.0, None, ALU.min).then_inc(v_dcol, 1)
                nc.vector.tensor_scalar(degc[:], deg[:], 1.0, None, ALU.max).then_inc(v_dcol, 1)
                done(3)
                nc.vector.tensor_scalar(noedge[:], ind[:, 0], -1.0, 1.0, ALU.mult, ALU.add).then_inc(v_dcol, 1)
                nc.vector.reciprocal(rdeg[:], degc[:]).then_inc(v_dcol, 1)
                for half in range(2):
                    nc.vector.tensor_copy(dcol[:, :, half, 0:2],
                                          deg[:].rearrange("p k t -> p t k")).then_inc(v_dcol, 1)
                    nc.vector.tensor_copy(dcol[:, :, half, 2:4],
                                          ind[:].rearrange("p k t -> p t k")).then_inc(v_dcol, 1)
                done(5)
                nc.vector.tensor_scalar(rdeg_h[:, t.par], rdeg[:], 1.0 / H_SCALE, None, ALU.mult).then_inc(v_dcol, 1)
                nc.vector.tensor_tensor(edges[:], mask[:, 0:TILES],
                                        noedge[:].unsqueeze(2).broadcast_to([P, TILES, N]),
                                        ALU.add).then_inc(v_dcol, 1)

            def residual0(t, i):
                dve.wait_ge(x1_full, t.count(4, i + 1))
                dve.wait_ge(g_xb, t.count(4, i + 1))
                nc.vector.tensor_tensor(x1[:, t.par, i], ps((J_X1A if i < 2 else J_X1B - 2) + i, D),
                                        x1[:, t.par, i], ALU.add).then_inc(v_x1, 1)
                dve.wait_ge(v_x1, t.count(4, i + 1))
                nc.vector.bn_stats(st6[:, 1, i], x1[:, t.par, i]).then_inc(v_st, 1)
                dve.wait_ge(v_st, t.count(4, i + 1))
                nc.vector.memset(spacer[:], 0.0)
                nc.vector.bn_aggr(mv[:, 1, i], st6[:, 1, i]).then_inc(v_mv, 1)
                dve.wait_ge(v_mv, t.count(4, i + 1))
                nc.vector.tensor_scalar(ve[:, 1, i:i + 1], mv[:, 1, i, 1:2], EPS, H_SCALE ** -2, ALU.add,
                                        ALU.mult).then_inc(v_ve, 1)

            def norm1_shift(t, i):
                dve.wait_ge(g_rstd, t.count(4, i + 1))
                nc.vector.scalar_tensor_tensor(out=nmr[:, 1, i:i + 1], in0=mv[:, 1, i, 0:1], scalar=-1.0,
                                               in1=rstd[:, 1, i:i + 1], op0=ALU.mult, op1=ALU.mult).then_inc(v_nmr, 1)

            def split_h2(t, i):
                dve.wait_ge(s_h2_hi, t.count(4, i + 1))
                nc.vector.tensor_tensor(h2_lo[:, i], h[:, i], h2_hi[:, i], ALU.subtract).then_inc(v_h2_lo, 1)

            def read_scores(t):
                dve.wait_ge(att_full, t.count(1, 1))
                for g in range(2):
                    r = slice(g * N, (g + 1) * N)
                    att = bank[J_T2 % 8][r].rearrange("p (t j) -> p t j", t=TILES)[:, :, r]
                    nc.vector.tensor_tensor(a[r].rearrange("p (m t) j -> p m t j", m=2),
                                            att.unsqueeze(1).broadcast_to([N, 2, TILES, N]),
                                            mask[r].rearrange("p (m t) j -> p m t j", m=2),
                                            ALU.mult).then_inc(v_a, 1)

            def shift_scores(t):
                dve.wait_ge(v_a, t.count(4, 2))
                nc.vector.tensor_tensor(a[:], a[:], neg[:], ALU.add).then_inc(v_a, 1)
                dve.wait_ge(v_a, t.count(4, 3))
                nc.vector.tensor_reduce(amax[:], a[:], AX.X, ALU.max).then_inc(v_f, 1)
                dve.wait_ge(v_f, t.count(8, 1))
                nc.vector.tensor_tensor(a[:], a[:], amax[:].unsqueeze(2).broadcast_to([P, 2 * TILES, N]),
                                        ALU.subtract).then_inc(v_a, 1)

            def weights(t):
                dve.wait_ge(s_exp, t.count(1, 1))
                nc.vector.tensor_reduce(esum[:], e[:], AX.X, ALU.add).then_inc(v_f, 1)
                dve.wait_ge(v_f, t.count(8, 2))
                nc.vector.reciprocal(rsum[:], esum[:]).then_inc(v_f, 1)
                dve.wait_ge(v_f, t.count(8, 3))
                nc.vector.tensor_tensor(rsd[:], rsum[:, 0:TILES], rdeg[:, 0], ALU.mult).then_inc(v_f, 1)
                dve.wait_ge(v_f, t.count(8, 4))
                nc.vector.tensor_tensor(z[:], e[:, 0:TILES], rsd[:].unsqueeze(2).broadcast_to([P, TILES, N]),
                                        ALU.mult).then_inc(v_f, 1)
                for g in range(2):
                    r = slice(g * N, (g + 1) * N)
                    last = nc.vector.tensor_tensor(An[r, :, r], e[r, TILES:],
                                                   rsum[r, TILES:].unsqueeze(2).broadcast_to([N, TILES, N]),
                                                   ALU.mult)
                last.then_inc(v_An, 1)

            def fusion(t):
                dve.wait_ge(s_zexp, t.count(1, 1))
                nc.vector.tensor_tensor(zm[:], zx[:], edges[:], ALU.mult).then_inc(v_f, 1)
                dve.wait_ge(v_f, t.count(8, 6))
                nc.vector.tensor_reduce(fsum[:], zm[:], AX.X, ALU.add).then_inc(v_f, 1)
                dve.wait_ge(v_f, t.count(8, 7))
                nc.vector.reciprocal(frec[:], fsum[:]).then_inc(v_f, 1)
                dve.wait_ge(v_f, t.count(8, 8))
                for g in range(2):
                    r = slice(g * N, (g + 1) * N)
                    last = nc.vector.tensor_tensor(Fn[r, :, r], zm[r],
                                                   frec[r].unsqueeze(2).broadcast_to([N, TILES, N]), ALU.mult)
                last.then_inc(v_Fn, 1)

            def split_fa(t, job, hi_ready, part, signal):
                dve.wait_ge(hi_ready, t.count(1, 1))
                nc.vector.scalar_tensor_tensor(out=fa_lo[:, :, part], in0=ps(job).rearrange("p (t i) -> p t i", t=TILES),
                                               scalar=F_SCALE, in1=fa_hi[:, :, part], op0=ALU.mult,
                                               op1=ALU.subtract).then_inc(signal, 1)

            def result(t, i):
                job = J_OUT + 3 * i if i < 3 else J_OUT3
                y = x1[:, t.par, i]
                dve.wait_ge(out_full, t.count(4, i + 1))
                nc.vector.scalar_tensor_tensor(out=y, in0=ps(job, D), scalar=1.0 / H_SCALE, in1=y,
                                               op0=ALU.mult, op1=ALU.add).then_inc(v_out_step, 1)
                dve.wait_ge(v_out_step, t.count(8, 2 * i + 1))
                nc.vector.scalar_tensor_tensor(out=y, in0=ps(job + 1, D), scalar=rdeg_h[:, t.par, 0, i:i + 1], in1=y,
                                               op0=ALU.mult, op1=ALU.add).then_inc(v_out_step, 1)
                dve.wait_ge(v_out_step, t.count(8, 2 * i + 2))
                nc.vector.scalar_tensor_tensor(out=y, in0=ps(job + 2, D), scalar=rdeg_h[:, t.par, 1, i:i + 1], in1=y,
                                               op0=ALU.mult, op1=ALU.add).then_inc(v_out, 1)

            def split_pair(t, job, k, hi_ready, scale, signal):
                dve.wait_ge(hi_ready, t.count(6, k + 1))
                part = slice(2 * (k % 2), 2 * (k % 2) + 2)
                nc.vector.scalar_tensor_tensor(out=yz_lo[:, k // 2, part],
                                               in0=bank[(job + k) % 8][:].rearrange("p (t i) -> p t i", t=2),
                                               scalar=scale, in1=yz_hi[:, k // 2, part].bitcast(F32),
                                               op0=ALU.mult, op1=ALU.subtract).then_inc(signal, 1)

            def turn(t):
                n, more = t.plus(1), not is_last(t, 1)
                for k in range(2 * C):
                    split_pair(t, J_YZ, k, s_yz_hi, 1.0 / (H_SCALE * F_SCALE), v_yz_lo)
                if more:
                    split_hT(n)
                    masks(n)
                residual0(t, 0)
                residual0(t, 1)
                norm1_shift(t, 0)
                norm1_shift(t, 1)
                split_h2(t, 0)
                if more:
                    degrees(n)
                split_h2(t, 1)
                residual0(t, 2)
                norm1_shift(t, 2)
                residual0(t, 3)
                norm1_shift(t, 3)
                split_h2(t, 2)
                split_h2(t, 3)
                if more:
                    read_scores(n)
                for c in range(C):
                    dve.wait_ge(s_h2T_hi, t.count(3, c + 1))
                    nc.vector.tensor_tensor(hT_lo[:, c], ps(J_H2T + c), hT_hi[:, c].bitcast(F32),
                                            ALU.subtract).then_inc(v_h2T_lo, 1)
                for k in range(2 * C):
                    split_pair(t, J_AGG, k, s_agg_hi, 1.0, v_agg_lo)
                if more:
                    shift_scores(n)
                if not is_last(t, 2):
                    norm0_stats(t.plus(2))
                if more:
                    weights(n)
                result(t, 0)
                if more:
                    fusion(n)
                if not is_last(t, 2):
                    norm0_shift(t.plus(2))
                result(t, 1)
                result(t, 2)
                if more:
                    split_fa(n, J_FT, s_fT_hi, slice(0, P), v_fT_lo)
                    split_fa(n, J_AT, s_af_hi, slice(P, 2 * P), v_af_lo)
                result(t, 3)

            first = Turn(0, 0)
            norm0_stats(first)
            norm0_shift(first)
            dve.wait_ge(c_in, 16 * 18)
            dve.wait_ge(consts_ready, 8)
            nc.vector.tensor_copy(b3m[:], b3c[:].unsqueeze(2).broadcast_to([P, C, P])).then_inc(prep_dve, 1)
            for k in range(2):
                nc.vector.tensor_copy(relL[:, k, k:k + LO + 1:LO],
                                      relE[:, k:k + 1].broadcast_to([P, 2])).then_inc(prep_dve, 1)

            def split_weight(name):
                for c in range(C):
                    dve.wait_ge(prep_hi, names.index(name) * C + c + 1)
                    nc.vector.tensor_tensor(w_lo[name][:, c], prep_bank(name, c), w_hi[name][:, c].bitcast(F32),
                                            ALU.subtract).then_inc(prep_lo, 1)

            split_weight("G")
            dve.wait_ge(prep_full, FULL["b1W2"])
            nc.vector.tensor_scalar(tb[:], bank[3][:, 0:C], H_SCALE, None, ALU.mult).then_inc(prep_dve, 1)
            for c in range(C):
                dve.wait_ge(prep_full, FULL["W4T"] + c)
                nc.vector.tensor_copy(W4T[:, c], prep_bank("W4T", c)).then_inc(prep_dve, 1)
            split_weight("W34T")
            nc.vector.tensor_tensor(bias0[:], bias0[:], b4bc[:], ALU.add).then_inc(prep_dve, 1)
            dve.wait_ge(prep_full, FULL["bias"])
            dve.wait_ge(prep_dve, 8)
            nc.vector.tensor_tensor(bias0[:], bank[3][:, 0:D], bias0[:], ALU.add).then_inc(prep_dve, 1)
            split_weight("W3T")
            for k, b in enumerate((7, 3)):
                dve.wait_ge(prep_full, FULL["WrT"] + k)
                nc.vector.tensor_copy(WrTs[:, k], bank[b][:, 0:D]).then_inc(prep_dve, 1)
            split_weight("WadjT")
            dve.wait_ge(prep_full, FULL["rows"])
            nc.vector.tensor_tensor(rows[:], bank[7][0:64, 0:D], rows_b[:], ALU.add).then_inc(prep_dve, 1)
            dve.wait_ge(prep_dve, 12)
            nc.vector.tensor_scalar(rows[:], rows[:], H_SCALE, None, ALU.mult).then_inc(prep_dve, 1)
            dve.wait_ge(prep_dve, 13)
            nc.vector.tensor_copy(rows_r[:], rows[:]).then_inc(prep_dve, 1)
            nc.vector.tensor_copy(rank[0:LO], rows[0:LO]).then_inc(prep_dve, 1)
            dve.wait_ge(prep_dve, 14)
            nc.vector.tensor_tensor(rank[LO:64], rows[LO:64], rows_r[LO:64].bitcast(F32),
                                    ALU.subtract).then_inc(prep_dve, 1)
            split_weight("WrevT")
            split_weight("WselfT")
            masks(first)
            split_hT(first)
            degrees(first)
            read_scores(first)
            shift_scores(first)
            weights(first)
            norm0_stats(Turn(0, 1))
            norm0_shift(Turn(0, 1))
            fusion(first)
            split_fa(first, J_FT, s_fT_hi, slice(0, P), v_fT_lo)
            split_fa(first, J_AT, s_af_hi, slice(P, 2 * P), v_af_lo)
            turns(dve, turn, turn)

        @block.tensor
        def _(pe):
            def chunk(c):
                return slice(c * P, (c + 1) * P)

            def group(to, products):
                for k, (lhsT, rhs) in enumerate(products):
                    last = nc.tensor.matmul(to, lhsT, rhs, start=(k == 0), stop=(k == len(products) - 1))
                return last

            def three(l_hi, l_lo, r_hi, r_lo):
                return [(l_hi, r_hi), (l_hi, r_lo), (l_lo, r_hi)]

            def turn_h(t, job, signal):
                for c in range(C):
                    if c == 2:
                        wait(pe, v_yz_lo, t.count(6, -5))
                    for i in range(TILES):
                        last = nc.tensor.transpose(ps(job + c)[:, chunk(i)], h[:, i, chunk(c)], id32[:])
                    last.then_inc(signal, 1)

            def hT_job(t):
                pe.wait_ge(s_h, t.count(4, 4))
                wait(pe, v_out, t.count(4, -4))
                turn_h(t, J_HT, hT_full)

            def t_job(t, c):
                if c == 0:
                    pe.wait_ge(v_hT_lo, t.count(3, 3))
                    wait(pe, v_yz_lo, t.count(6, -3))
                g = [three(w_hi["G"][:, d, chunk(c)], w_lo["G"][:, d, chunk(c)], hT_hi[:, d], hT_lo[:, d])
                     for d in range(C)]
                group(ps(J_T + c if c < 2 else J_T2), sum(g, [])).then_inc(t_full, 1)

            def adjT_job(t):
                pe.wait_ge(v_adj, t.count(7, 7))
                to = bank[J_ADJT % 8][:].bitcast(F16)
                for i in range(TILES):
                    last = nc.tensor.transpose(to[:, chunk(i)], adj_b[:, t.par, i, P:2 * P], id16[:])
                last.then_inc(adjT_full, 1)

            def drow_job(t):
                pe.wait_ge(v_dcol, t.count(11, 11))
                pe.wait_ge(s_adjT, t.count(1, 1))
                to = bank[J_ADJT % 8][:].bitcast(F16)
                for i in range(TILES):
                    last = nc.tensor.transpose(to[:, W + i * P:W + (i + 1) * P],
                                               dcol[:, i].rearrange("p a b -> p (a b)"), id16[:])
                last.then_inc(drow_full, 1)

            def att_job(t):
                pe.wait_ge(s_tT, t.count(3, 3))
                for i in range(TILES):
                    last = group(ps(J_T2)[:, chunk(i)], [(tT[:, c, chunk(i)], hT[:, c, chunk(i)]) for c in range(C)])
                last.then_inc(att_full, 1)

            def fT_job(t):
                pe.wait_ge(v_Fn, t.count(1, 1))
                for i in range(TILES):
                    last = nc.tensor.transpose(ps(J_FT)[:, chunk(i)], Fn[:, i], id32[:])
                last.then_inc(fT_full, 1)
                for i in range(TILES):
                    last = nc.tensor.transpose(ps(J_AT)[:, chunk(i)], An[:, i], id32[:])
                last.then_inc(aT_full, 1)

            def af_job(t):
                pe.wait_ge(s_AT, t.count(1, 1))
                for i in range(TILES):
                    last = group(ps(J_AT)[:, chunk(i)], [(Fn[:, i], AT[:, i])])
                last.then_inc(af_full, 1)

            def x1_job(t, i):
                if i == 0:
                    pe.wait_ge(v_yz_lo, t.count(6, 6))
                y, zz = slice(0, P), slice(P, 2 * P)
                g = [three(yz_hi[:, c, i, part], yz_lo[:, c, i, part], w_hi[w][:, c], w_lo[w][:, c])
                     for w, part in (("W3T", y), ("W34T", zz)) for c in range(C)]
                group(ps((J_X1A if i < 2 else J_X1B - 2) + i, D), sum(g, [])).then_inc(x1_full, 1)

            def self_job(t, i, job):
                g = [three(hT_hi[:, c, chunk(i)], hT_lo[:, c, chunk(i)], w_hi["WselfT"][:, c], w_lo["WselfT"][:, c])
                     for c in range(C)]
                return group(ps(job, D), sum(g, [(drow[:, t.par, chunk(i)], rank[:])]))

            def agg_job(i, job, part, w):
                g = [three(yz_hi[:, c, i, part], yz_lo[:, c, i, part], w_hi[w][:, c], w_lo[w][:, c]) for c in range(C)]
                return group(ps(job, D), sum(g, []))

            def turn(t):
                n, more = t.plus(1), not is_last(t, 1)
                pe.wait_ge(v_fT_lo, t.count(1, 1))
                pe.wait_ge(v_af_lo, t.count(1, 1))
                pe.wait_ge(g_h_lo, t.count(4, 4))
                wait(pe, v_out, t.count(4, -1))
                for k in range(2 * C):
                    if k == 2 * C - 1:
                        wait(pe, v_out, t.count(4, 0))
                    for half in range(2):
                        i, c = 2 * (k % 2) + half, k // 2
                        last = group(ps(J_YZ + k)[:, half * 2 * P:(half + 1) * 2 * P],
                                     three(h_hi[:, t.par, i, chunk(c)], h_lo[:, t.par, i, chunk(c)],
                                           fa_hi[:, i], fa_lo[:, i]))
                    last.then_inc(yz_full, 1)
                if more:
                    hT_job(n)
                    t_job(n, 0)
                    t_job(n, 1)
                x1_job(t, 0)
                x1_job(t, 1)
                if more:
                    adjT_job(n)
                x1_job(t, 2)
                x1_job(t, 3)
                if more:
                    t_job(n, 2)
                    drow_job(n)
                    att_job(n)
                pe.wait_ge(s_h2, t.count(4, 4))
                for c in range(C):
                    if c == 2:
                        pe.wait_ge(v_x1, t.count(4, 1))
                    for i in range(TILES):
                        last = nc.tensor.transpose(ps(J_H2T + c)[:, chunk(i)], h[:, i, chunk(c)], id32[:])
                    last.then_inc(h2T_full, 1)
                pe.wait_ge(s_h2_hi, t.count(4, 4))
                pe.wait_ge(v_h2_lo, t.count(4, 4))
                pe.wait_ge(s_adjT, t.count(1, 1))
                for k in range(2 * C):
                    if k == 1 and more:
                        pe.wait_ge(s_drow, n.count(1, 1))
                    if k == 4 and more:
                        pe.wait_ge(v_a, n.count(4, 2))
                    if k == 5:
                        pe.wait_ge(v_h2T_lo, t.count(3, 1))
                    for half in range(2):
                        i, c = 2 * (k % 2) + half, k // 2
                        last = group(ps(J_AGG + k)[:, half * 2 * P:(half + 1) * 2 * P],
                                     [(h2_hi[:, i, chunk(c)], adj_b[:, t.par, i]),
                                      (h2_lo[:, i, chunk(c)], adj_b[:, t.par, i])])
                    last.then_inc(agg_full, 1)
                pe.wait_ge(v_h2T_lo, t.count(3, 3))
                pe.wait_ge(s_drow, t.count(1, 1))
                for i in range(TILES):
                    job = J_OUT + 3 * i if i < 3 else J_OUT3
                    if i == 3 and more:
                        fT_job(n)
                    if i == 3:
                        pe.wait_ge(v_out, t.count(4, 2))
                    self_job(t, i, job)
                    if i == 0:
                        pe.wait_ge(v_agg_lo, t.count(6, 6))
                    agg_job(i, job + 1, slice(0, P), "WadjT")
                    if i == 3 and more:
                        af_job(n)
                    if i == 2:
                        pe.wait_ge(v_out, t.count(4, 1))
                    agg_job(i, job + 2, slice(P, 2 * P), "WrevT").then_inc(out_full, 1)

            def transposed(name, natural_w):
                for c in range(C):
                    for o in range(C):
                        last = nc.tensor.transpose(prep_bank(name, c)[:, chunk(o)], natural_w[:, o, chunk(c)], id32[:])
                    last.then_inc(prep_full, 1)

            pe.wait_ge(ident_ready, 2)
            pe.wait_ge(w_in[0], 32)
            for c in range(C):
                group(prep_bank("G", c), [(W1n[:, o, chunk(c)], W2n[:, o]) for o in range(C)]).then_inc(prep_full, 1)
            pe.wait_ge(c_in, 16 * 18)
            for c in range(C):
                last = group(bank[3][:, c:c + 1], [(W2n[:, o, chunk(c)], b1c[:, o:o + 1]) for o in range(C)])
            last.then_inc(prep_full, 1)
            pe.wait_ge(w_in[1], 32)
            transposed("W4T", W4n)
            pe.wait_ge(prep_dve, 7)
            pe.wait_ge(prep_lo, 3)
            for c in range(C):
                group(prep_bank("W34T", c), [(W3n[:, o, chunk(c)], W4T[:, o]) for o in range(C)]).then_inc(prep_full, 1)
            group(bank[3][:, 0:D], [(b3m[:, o], W4T[:, o]) for o in range(C)]).then_inc(prep_full, 1)
            transposed("W3T", W3n)
            for k, b in enumerate((7, 3)):
                if k == 1:
                    pe.wait_ge(prep_dve, 9)
                for o in range(C):
                    last = nc.tensor.transpose(bank[b][:, chunk(o)], WrN[:, k, o], id32[:])
                last.then_inc(prep_full, 1)
            pe.wait_ge(w_in[2], 16)
            pe.wait_ge(prep_lo, 6)
            transposed("WadjT", W1n)
            pe.wait_ge(prep_dve, 11)
            group(bank[7][0:64, 0:D], [(relL[:, k], WrTs[:, k]) for k in range(2)]).then_inc(prep_full, 1)
            pe.wait_ge(w_in[3], 16)
            pe.wait_ge(prep_lo, 9)
            transposed("WrevT", W2n)
            pe.wait_ge(w_in[4], 16)
            pe.wait_ge(prep_lo, 12)
            transposed("WselfT", W3n)
            first = Turn(0, 0)
            pe.wait_ge(prep_lo, 18)
            pe.wait_ge(prep_dve, 16)
            hT_job(first)
            for c in range(C):
                t_job(first, c)
            adjT_job(first)
            drow_job(first)
            att_job(first)
            fT_job(first)
            af_job(first)
            turns(pe, turn, turn)


INPUTS = ("x", "adj", "L0_gnn_W1", "L0_gnn_b1", "L0_gnn_W2", "L0_gnn_b2", "L0_gnn_W3", "L0_gnn_b3", "L0_gnn_W4",
          "L0_gnn_b4", "L1_gnn_E", "L1_gnn_Wadj", "L1_gnn_badj", "L1_gnn_Wrev", "L1_gnn_brev", "L1_gnn_Wself",
          "L1_gnn_bself", "L1_gnn_Wr", "L1_gnn_br", "L1_gnn_Wrr", "L1_gnn_brr")


def kernel(**inputs):
    import numpy as np
    import concourse.bacc as bacc
    from concourse.bass_utils import run_bass_kernel_spmd

    nc = bacc.Bacc("TRN2", target_bir_lowering=False, num_devices=1)
    arrays, d = {}, {}
    for name in INPUTS:
        v = np.ascontiguousarray(inputs[name])
        arrays[f"in_{name}"] = v
        d[name] = nc.dram_tensor(f"in_{name}", v.shape, mybir.dt.from_np(v.dtype), kind="ExternalInput").ap()
    out = nc.dram_tensor("out", (GRAPHS, N, D), F32, kind="ExternalOutput").ap()
    a, b = "L0_gnn_", "L1_gnn_"
    build(nc, d["x"], d["adj"], [d[a + w] for w in ("W1", "W2", "W3", "W4")],
          [d[a + w] for w in ("b1", "b2", "b3", "b4")], d[b + "E"],
          [d[b + w] for w in ("Wadj", "Wrev", "Wself")], [d[b + w] for w in ("badj", "brev", "bself")],
          d[b + "Wr"], d[b + "br"], d[b + "Wrr"], d[b + "brr"], out)
    r = run_bass_kernel_spmd(nc, [arrays], core_ids=[0])
    return r.results[0]["out"]
```

```python
from contextlib import ExitStack

import concourse.bass as bass
from concourse import mybir

F32 = mybir.dt.float32
F32R = mybir.dt.float32r
F16 = mybir.dt.float16
I32 = mybir.dt.int32
ALU = mybir.AluOpType
ACT = mybir.ActivationFunctionType
AX = mybir.AxisListType

P = 128
GRAPHS, N, D = 128, 64, 384
TILES = 4
W = TILES * P
ST = GRAPHS * N // W
C = D // P
R = 128
REL, REL_REV = 1, 41
EPS = 1e-5
H_SCALE = 64.0
F_SCALE = 1024.0
ATT_SCALE = 1.0 / (28.0 * H_SCALE * H_SCALE)
BIG = 1e9 / ATT_SCALE
LO = 32

J_YZ = 0
J_T = (6, 7, 13)
J_X1 = (8, 9, 11, 12)
J_ADJT = 10
J_ATT = 13
J_AGG = (14, 15, 16, 20, 21, 22)
J_H2T = 17
J_SELF, J_ADJ, J_REV = (25, 26, 29, 34), (23, 27, 30, 35), (24, 28, 31, 39)
J_FT, J_AT = 32, 33
J_HT = 36
N_SELF, N_ADJ, N_REV = (3, 4, 7, 10), (1, 5, 8, 11), (2, 6, 9, 12)


class Turn:

    def __init__(self, it, u):
        self.it, self.u = it, u

    def plus(self, n):
        return Turn(self.it, self.u + n)

    @property
    def par(self):
        return self.u % 2

    @property
    def index(self):
        return self.it * 2 + self.u

    def count(self, per, k):
        return self.it * (2 * per) + (self.u * per + k)

    def dma(self, per, k):
        return (self.it + self.u // 2) * (16 * per) + 16 * k


def wait(eng, sem, value):
    if isinstance(value, int) and value <= 0:
        return
    eng.wait_ge(sem, value)


def build(nc, x, adj, w0, b0, E, w1, b1, Wr, br, Wrr, brr, out):
    W1, W2, W3, W4 = w0
    Wadj, Wrev, Wself = w1

    x_v = x.rearrange("(s t h) n d -> s (h n) t d", t=TILES, h=2)
    out_v = out.rearrange("(s t h) n d -> s (h n) t d", t=TILES, h=2)
    adj_v = adj.rearrange("(s t h) i j -> s (h i) t j", t=TILES, h=2)

    with ExitStack() as ctx:
        def sb(name, shape, dt=F32):
            return ctx.enter_context(nc.sbuf_tensor(name, shape, dt))

        def sem(name):
            return ctx.enter_context(nc.semaphore(name))

        bank = [ctx.enter_context(nc.psum_tensor(f"bank{i}", [P, 512], F32)) for i in range(8)]

        def ps(job, n=512):
            return bank[job % 8][:, 0:n]

        names = ("G", "W34T", "W3T", "WadjT", "WrevT", "WselfT")
        w_hi = {k: sb(k + "_hi", [P, C, D], F32R) for k in names}
        w_lo = {k: sb(k + "_lo", [P, C, D], F32R) for k in names}
        W4T = sb("W4T", [P, C, D])
        relE = sb("relE", [P, 2])
        relL = sb("relL", [P, 2, 64])
        b1c = sb("b1c", [P, C])
        b3c = sb("b3c", [P, C])
        b3m = sb("b3m", [P, C, P])
        tb = sb("tb", [P, C])
        bias0 = sb("bias0", [P, D])
        b4bc = sb("b4bc", [P, D])
        rows = sb("rows", [64, D])
        rows_b = sb("rows_b", [64, D])
        rows_r = sb("rows_r", [64, D], F32R)
        rank = sb("rank", [64, D], F32R)
        id32 = sb("id32", [P, P])
        id16 = sb("id16", [P, P], F16)
        minus_half = sb("minus_half", [P, TILES])

        xin = sb("xin", [P, 2, TILES, D])
        x1 = sb("x1", [P, 2, TILES, D])
        h = sb("h", [P, TILES, D])
        h_hi = sb("h_hi", [P, 2, TILES, D], F16)
        h_lo = sb("h_lo", [P, 2, TILES, D], F16)
        h2_hi = sb("h2_hi", [P, TILES, D], F16)
        h2_lo = sb("h2_lo", [P, TILES, D], F16)
        hT = sb("hT", [P, C, W])
        hT_hi = sb("hT_hi", [P, C, W], F32R)
        hT_lo = sb("hT_lo", [P, C, W], F32R)
        tT = sb("tT", [P, C, W])
        yz_hi = sb("yz_hi", [P, C, TILES, 2 * P], F32R)
        yz_lo = sb("yz_lo", [P, C, TILES, 2 * P], F32R)
        st6 = sb("st6", [P, 2, TILES, 6])
        mv = sb("mv", [P, 2, TILES, 2])
        ve = sb("ve", [P, 2, TILES])
        rstd = sb("rstd", [P, 2, TILES])
        nmr = sb("nmr", [P, 2, TILES])
        spacer = sb("spacer", [P, 1])
        adj_i = sb("adj_i", [P, 2, TILES, N], I32)
        mask = sb("mask", [P, 2 * TILES, N])
        neg = sb("neg", [P, 2 * TILES, N])
        edges = sb("edges", [P, TILES, N])
        adj_b = sb("adj_b", [P, 2, TILES, 2 * P], F16)
        deg = sb("deg", [P, 2, TILES])
        ind = sb("ind", [P, 2, TILES])
        noedge = sb("noedge", [P, TILES])
        degc = sb("degc", [P, 2, TILES])
        rdeg = sb("rdeg", [P, 2, TILES])
        rdeg_h = sb("rdeg_h", [P, 2, 2, TILES])
        dcol = sb("dcol", [P, TILES, 4, 32], F16)
        drow = sb("drow", [64, 2, W], F32R)
        sc = sb("sc", [P, TILES, N])
        a = sb("a", [P, 2 * TILES, N])
        e = sb("e", [P, 2 * TILES, N])
        amax = sb("amax", [P, 2 * TILES])
        esum = sb("esum", [P, 2 * TILES])
        rsum = sb("rsum", [P, 2 * TILES])
        rsd = sb("rsd", [P, TILES])
        z = sb("z", [P, TILES, N])
        zx = sb("zx", [P, TILES, N])
        zm = sb("zm", [P, TILES, N])
        fsum = sb("fsum", [P, TILES])
        frec = sb("frec", [P, TILES])
        Fn = sb("Fn", [P, TILES, P])
        An = sb("An", [P, TILES, P])
        AT = sb("AT", [P, TILES, P])
        fa_hi = sb("fa_hi", [P, TILES, 2 * P], F16)
        fa_lo = sb("fa_lo", [P, TILES, 2 * P], F16)

        x1_flat = x1[:].rearrange("p a t d -> p (a t d)")

        def staged(flat, at=0):
            return flat[:, at:at + C * D].rearrange("p (c d) -> p c d", c=C)

        W1n, W2n = staged(x1_flat, 0), staged(x1_flat, C * D)
        W3n = sb("W3n", [P, C, D])[:]
        W4n = staged(xin[:, 1].rearrange("p t d -> p (t d)"))
        WrTs = x1_flat[:, 2 * C * D:2 * C * D + 2 * D].rearrange("p (k d) -> p k d", k=2)
        WrN = h2_hi[:].rearrange("p t d -> p (t d)").bitcast(F32).rearrange("p (k c r) -> p k c r", k=2, c=C)

        x_in = [sem("x_in0"), sem("x_in1")]
        adj_in = [sem("adj_in0"), sem("adj_in1")]
        out_sent = [sem("out_sent0"), sem("out_sent1")]
        w_in = [sem(f"w_in{i}") for i in range(5)]
        c_in = sem("c_in")
        ident_ready, consts_ready, zeros_ready = sem("ident_ready"), sem("consts_ready"), sem("zeros_ready")
        prep_dve, prep_full, prep_hi, prep_lo = sem("prep_dve"), sem("prep_full"), sem("prep_hi"), sem("prep_lo")
        yz_full = sem("yz_full")
        hT_full = sem("hT_full")
        t_full = sem("t_full")
        x1_full = sem("x1_full")
        adjT_full = sem("adjT_full")
        drow_full = sem("drow_full")
        att_full = sem("att_full")
        h2T_full = sem("h2T_full")
        agg_full = sem("agg_full")
        out_full = sem("out_full")
        fT_full = sem("fT_full")
        aT_full = sem("aT_full")
        af_full = sem("af_full")
        s_yz_hi = sem("s_yz_hi")
        s_hT_hi = sem("s_hT_hi")
        s_tT = sem("s_tT")
        s_h2 = sem("s_h2")
        s_h2_hi = sem("s_h2_hi")
        s_adjT = sem("s_adjT")
        s_drow = sem("s_drow")
        s_h2T_hi = sem("s_h2T_hi")
        s_agg_hi = sem("s_agg_hi")
        s_sc = sem("s_sc")
        s_exp = sem("s_exp")
        s_zexp = sem("s_zexp")
        s_h = sem("s_h")
        s_h_hi = sem("s_h_hi")
        s_fT_hi = sem("s_fT_hi")
        s_AT = sem("s_AT")
        s_af_hi = sem("s_af_hi")
        v_yz_lo = sem("v_yz_lo")
        v_hT_lo = sem("v_hT_lo")
        v_x1 = sem("v_x1")
        v_st = sem("v_st")
        v_mv = sem("v_mv")
        v_ve = sem("v_ve")
        v_nmr = sem("v_nmr")
        v_h2_lo = sem("v_h2_lo")
        v_h2T_lo = sem("v_h2T_lo")
        v_agg_lo = sem("v_agg_lo")
        v_adj = sem("v_adj")
        v_dcol = sem("v_dcol")
        v_a = sem("v_a")
        v_f = sem("v_f")
        v_An = sem("v_An")
        v_Fn = sem("v_Fn")
        v_st0 = sem("v_st0")
        v_mv0 = sem("v_mv0")
        v_ve0 = sem("v_ve0")
        v_nmr0 = sem("v_nmr0")
        v_fT_lo = sem("v_fT_lo")
        v_af_lo = sem("v_af_lo")
        v_out_step = sem("v_out_step")
        v_out = sem("v_out")
        g_xb = sem("g_xb")
        g_rstd = sem("g_rstd")
        g_rstd0 = sem("g_rstd0")
        g_h_lo = sem("g_h_lo")
        g_hT = sem("g_hT")

        FULL = {"G": 1, "b1W2": 4, "W4T": 5, "W34T": 8, "bias": 11, "W3T": 12, "WrT": 15, "WrrT": 16,
                "WadjT": 17, "rows": 20, "WrevT": 21, "WselfT": 24}

        PREP_BANK = {"G": (0, 1, 2), "b1W2": (3,), "W4T": (0, 1, 3), "W34T": (0, 1, 4), "bias": (3,),
                     "W3T": (6, 7, 0), "WrT": (1,), "WrrT": (4,), "WadjT": (3, 6, 7), "rows": (0,),
                     "WrevT": (1, 4, 2), "WselfT": (3, 6, 7)}

        def prep_bank(name, c=0, n=D):
            return bank[PREP_BANK[name][c]][:, 0:n]

        block = ctx.enter_context(nc.Block())

        def turns(eng, body, last):
            body(Turn(0, 0))
            body(Turn(0, 1))
            with eng.Fori(1, ST // 2 - 1) as it:
                body(Turn(it, 0))
                body(Turn(it, 1))
            body(Turn(ST // 2 - 1, 0))
            last(Turn(ST // 2 - 1, 1))

        def is_last(t, ahead):
            return isinstance(t.it, int) and t.index + ahead >= ST

        @block.sync
        def _(sp):
            def load(t):
                sp.dma_start(xin[:, t.par], x_v[t.index]).then_inc(x_in[t.par], 16)

            def load_adj(t):
                sp.dma_start(adj_i[:, t.par], adj_v[t.index]).then_inc(adj_in[t.par], 16)

            def natural(w):
                return w.rearrange("(c p) d -> p c d", p=P)

            sp.dma_start(W1n, natural(W1)).then_inc(w_in[0], 16)
            sp.dma_start(W2n, natural(W2)).then_inc(w_in[0], 16)
            load(Turn(0, 0))
            load_adj(Turn(0, 0))
            sp.dma_start(W4n, natural(W4)).then_inc(w_in[1], 16)
            sp.dma_start(W3n, natural(W3)).then_inc(w_in[1], 16)
            load_adj(Turn(0, 1))
            sp.wait_ge(prep_full, 3)
            sp.dma_start(W1n, natural(Wadj)).then_inc(w_in[2], 16)
            sp.wait_ge(prep_full, 4)
            sp.dma_start(W2n, natural(Wrev)).then_inc(w_in[3], 16)
            sp.wait_ge(prep_full, FULL["W4T"] + 2)
            load(Turn(0, 1))
            sp.wait_ge(prep_full, FULL["W3T"] + 2)
            sp.dma_start(W3n, natural(Wself)).then_inc(w_in[4], 16)

            def turn(t):
                if not is_last(t, 2):
                    sp.wait_ge(g_xb, t.count(4, 4))
                    load(t.plus(2))
                    sp.wait_ge(v_adj, t.count(7, 7))
                    load_adj(t.plus(2))
                for i in range(TILES):
                    wait(sp, v_out, t.count(4, i + 1))
                    sp.dma_start(out_v[t.index][:, i], x1[:, t.par, i]).then_inc(out_sent[t.par], 16)

            turns(sp, turn, turn)
            for par in range(2):
                sp.wait_ge(out_sent[par], 16 * TILES * ST // 2)

        @block.gpsimd
        def _(pool):
            nc.gpsimd.memset(id32[:], 0.0).then_inc(zeros_ready, 1)
            nc.gpsimd.memset(id16[:], 0.0).then_inc(zeros_ready, 1)
            pool.wait_ge(zeros_ready, 2)
            for m in (id32, id16):
                nc.gpsimd.affine_select(out=m[:], in_=m[:], compare_op=ALU.not_equal, fill=1.0, base=0,
                                        pattern=[[-1, P]], channel_multiplier=1).then_inc(ident_ready, 1)
            nc.gpsimd.memset(minus_half[:], -0.5).then_inc(consts_ready, 1)
            nc.gpsimd.memset(relL[:], 0.0).then_inc(consts_ready, 1)
            nc.gpsimd.memset(rows_b[:], 0.0).then_inc(consts_ready, 1)
            for m in (adj_b, Fn, An):
                nc.gpsimd.memset(m[:], 0.0).then_inc(consts_ready, 1)
            nc.gpsimd.memset(dcol[:], 0.0).then_inc(consts_ready, 1)
            pool.wait_ge(consts_ready, 7)
            nc.gpsimd.memset(dcol[:, :, 0:2, 4], 1.0).then_inc(consts_ready, 1)

            def rstd_of(t, ready, signal, ln, part):
                pool.wait_ge(*ready)
                nc.gpsimd.tensor_tensor(rstd[:, ln, part], ve[:, ln, part], minus_half[:, part],
                                        ALU.pow).then_inc(signal, 1)

            def norm0(t):
                wait(pool, s_h_hi, t.count(4, 0))
                rstd_of(t, (v_ve0, t.count(1, 1)), g_rstd0, 0, slice(0, TILES))
                wait(pool, yz_full, t.count(6, -6))
                for i in range(TILES):
                    pool.wait_ge(s_h_hi, t.count(4, i + 1))
                    nc.gpsimd.tensor_tensor(h_lo[:, t.par, i], h[:, i], h_hi[:, t.par, i],
                                            ALU.subtract).then_inc(g_h_lo, 1)

            def add_bias(t):
                wait(pool, out_sent[t.par], t.dma(4, 0))
                pool.wait_ge(x_in[t.par], t.dma(1, 1))
                for i in range(TILES):
                    nc.gpsimd.tensor_tensor(x1[:, t.par, i], xin[:, t.par, i], bias0[:], ALU.add).then_inc(g_xb, 1)

            def join_hT(t):
                for c in range(C):
                    pool.wait_ge(v_hT_lo, t.count(3, c + 1))
                    wait(pool, att_full, t.count(1, 0))
                    nc.gpsimd.tensor_tensor(hT[:, c], hT_hi[:, c].bitcast(F32), hT_lo[:, c].bitcast(F32),
                                            ALU.add).then_inc(g_hT, 1)

            def turn(t):
                if not is_last(t, 1):
                    join_hT(t.plus(1))
                    add_bias(t.plus(1))
                for i in range(TILES):
                    rstd_of(t, (v_ve, t.count(4, i + 1)), g_rstd, 1, slice(i, i + 1))
                if not is_last(t, 2):
                    norm0(t.plus(2))

            pool.wait_ge(consts_ready, 1)
            norm0(Turn(0, 0))
            join_hT(Turn(0, 0))
            norm0(Turn(0, 1))
            pool.wait_ge(prep_full, FULL["WrevT"] + 2)
            pool.wait_ge(prep_dve, 9)
            add_bias(Turn(0, 0))
            turns(pool, turn, turn)

        @block.scalar
        def _(act):
            def row(v):
                return v.rearrange("(a d) -> a d", a=1)

            act.dma_start(b1c[:], b0[0].rearrange("(c p) -> p c", p=P), allow_slow_non_contiguous=True).then_inc(c_in, 16)
            act.dma_start(b3c[:], b0[2].rearrange("(c p) -> p c", p=P), allow_slow_non_contiguous=True).then_inc(c_in, 16)
            act.dma_start(bias0[:], row(b0[2]).broadcast_to([P, D])).then_inc(c_in, 16)
            act.dma_start(b4bc[:], row(b0[3]).broadcast_to([P, D])).then_inc(c_in, 16)
            act.dma_start(relE[:, 0:1], E[REL:REL + 1, :].rearrange("a r -> r a"), allow_slow_non_contiguous=True).then_inc(c_in, 16)
            act.dma_start(relE[:, 1:2], E[REL_REV:REL_REV + 1, :].rearrange("a r -> r a"), allow_slow_non_contiguous=True).then_inc(c_in, 16)
            act.dma_start(WrN[:, 0], Wr.rearrange("(c p) r -> p c r", p=P)).then_inc(c_in, 16)
            act.dma_start(WrN[:, 1], Wrr.rearrange("(c p) r -> p c r", p=P)).then_inc(c_in, 16)
            for part in (0, LO):
                act.wait_ge(consts_ready, 3)
                for k, v in enumerate((br, brr, b1[0], b1[1], b1[2])):
                    act.dma_start(rows_b[part + k:part + k + 1, :], row(v)).then_inc(c_in, 16)

            def norm0(t):
                act.wait_ge(x_in[t.par], t.dma(1, 1))
                act.wait_ge(v_nmr0, t.count(1, 1))
                wait(act, v_h2_lo, t.count(4, -4))
                wait(act, g_h_lo, t.count(4, 0))
                for i in range(TILES):
                    nc.scalar.activation(h[:, i], xin[:, t.par, i], ACT.Relu, bias=nmr[:, 0, i:i + 1],
                                         scale=rstd[:, 0, i:i + 1]).then_inc(s_h, 1)
                for i in range(TILES):
                    act.wait_ge(s_h, t.count(4, i + 1))
                    nc.scalar.activation(h_hi[:, t.par, i], h[:, i], ACT.Copy).then_inc(s_h_hi, 1)

            def copy_hT(t):
                for c in range(C):
                    act.wait_ge(hT_full, t.count(3, c + 1))
                    nc.scalar.activation(hT_hi[:, c], ps(J_HT + c), ACT.Copy).then_inc(s_hT_hi, 1)

            def copy_tT(t, c):
                act.wait_ge(t_full, t.count(3, c + 1))
                nc.scalar.activation(tT[:, c], ps(J_T[c]), ACT.Identity,
                                     bias=tb[:, c:c + 1]).then_inc(s_tT, 1)

            def copy_adjT(t):
                act.wait_ge(v_dcol, t.count(11, 1))
                nc.scalar.activation(adj_b[:, t.par, :, 0:P],
                                     bank[J_ADJT % 8][:].bitcast(F16)[:, 0:W].rearrange("p (t i) -> p t i", t=TILES),
                                     ACT.Copy).then_inc(s_adjT, 1)

            def copy_drow(t):
                act.wait_ge(drow_full, t.count(1, 1))
                nc.scalar.activation(drow[:, t.par], bank[J_ADJT % 8][0:64].bitcast(F16)[:, W:2 * W],
                                     ACT.Copy).then_inc(s_drow, 1)

            def norm1(t, i):
                act.wait_ge(v_nmr, t.count(4, i + 1))
                if i == 0 and not is_last(t, 1):
                    wait(act, g_h_lo, t.plus(1).count(4, 4))
                nc.scalar.activation(h[:, i], x1[:, t.par, i], ACT.Relu, bias=nmr[:, 1, i:i + 1],
                                     scale=rstd[:, 1, i:i + 1]).then_inc(s_h2, 1)
                act.wait_ge(s_h2, t.count(4, i + 1))
                nc.scalar.activation(h2_hi[:, i], h[:, i], ACT.Copy).then_inc(s_h2_hi, 1)

            def copy_scores(t):
                act.wait_ge(att_full, t.count(1, 1))
                for g in range(2):
                    r = slice(g * N, (g + 1) * N)
                    last = nc.scalar.activation(sc[r], bank[J_ATT % 8][r].rearrange("p (t j) -> p t j", t=TILES)[:, :, r],
                                                ACT.Copy)
                last.then_inc(s_sc, 1)

            def exp_scores(t):
                act.wait_ge(v_a, t.count(3, 3))
                nc.scalar.activation(e[:], a[:], ACT.Exp, scale=ATT_SCALE).then_inc(s_exp, 1)

            def exp_fusion(t):
                act.wait_ge(v_f, t.count(8, 5))
                nc.scalar.activation(zx[:], z[:], ACT.Exp).then_inc(s_zexp, 1)

            def copy_fT(t):
                act.wait_ge(fT_full, t.count(1, 1))
                nc.scalar.activation(fa_hi[:, :, 0:P], ps(J_FT).rearrange("p (t i) -> p t i", t=TILES),
                                     ACT.Copy, scale=F_SCALE).then_inc(s_fT_hi, 1)
                act.wait_ge(aT_full, t.count(1, 1))
                nc.scalar.activation(AT[:], ps(J_AT).rearrange("p (t i) -> p t i", t=TILES),
                                     ACT.Copy).then_inc(s_AT, 1)

            def copy_af(t):
                act.wait_ge(af_full, t.count(1, 1))
                nc.scalar.activation(fa_hi[:, :, P:2 * P], ps(J_AT).rearrange("p (t i) -> p t i", t=TILES),
                                     ACT.Copy, scale=F_SCALE).then_inc(s_af_hi, 1)

            def pair(job):
                return bank[job % 8][:].rearrange("p (t i) -> p t i", t=2)

            def turn(t):
                n = t.plus(1)
                more = not is_last(t, 1)
                for k in range(2 * C):
                    act.wait_ge(yz_full, t.count(6, k + 1))
                    nc.scalar.activation(yz_hi[:, k // 2, 2 * (k % 2):2 * (k % 2) + 2], pair(J_YZ + k), ACT.Copy,
                                         scale=1.0 / (H_SCALE * F_SCALE)).then_inc(s_yz_hi, 1)
                if more:
                    copy_tT(n, 0)
                    copy_tT(n, 1)
                norm1(t, 0)
                norm1(t, 1)
                if more:
                    copy_adjT(n)
                norm1(t, 2)
                if more:
                    copy_drow(n)
                    copy_tT(n, 2)
                norm1(t, 3)

                def copy_agg(k):
                    act.wait_ge(agg_full, t.count(6, k + 1))
                    nc.scalar.activation(yz_hi[:, k % C, 2 * (k // C):2 * (k // C) + 2], pair(J_AGG[k]),
                                         ACT.Copy).then_inc(s_agg_hi, 1)

                for k in range(C):
                    copy_agg(k)
                if more:
                    copy_scores(n)
                for c in range(C):
                    act.wait_ge(h2T_full, t.count(3, c + 1))
                    nc.scalar.activation(hT_hi[:, c], ps(J_H2T + c), ACT.Copy).then_inc(s_h2T_hi, 1)
                for k in range(C, 2 * C):
                    copy_agg(k)
                if more:
                    exp_scores(n)
                    exp_fusion(n)
                if not is_last(t, 2):
                    norm0(t.plus(2))
                if more:
                    copy_fT(n)
                    copy_af(n)
                if not is_last(t, 2):
                    copy_hT(t.plus(2))

            norm0(Turn(0, 0))

            def copy_weight(name):
                for c in range(C):
                    act.wait_ge(prep_full, FULL[name] + c)
                    nc.scalar.activation(w_hi[name][:, c], prep_bank(name, c), ACT.Copy).then_inc(prep_hi, 1)

            first = Turn(0, 0)
            copy_weight("G")
            copy_hT(first)
            act.wait_ge(prep_dve, 4)
            for c in range(C):
                copy_tT(first, c)
            copy_weight("W34T")
            copy_adjT(first)
            copy_weight("W3T")
            copy_drow(first)
            copy_scores(first)
            copy_weight("WadjT")
            exp_scores(first)
            copy_weight("WrevT")
            exp_fusion(first)
            norm0(Turn(0, 1))
            copy_weight("WselfT")
            copy_fT(first)
            copy_af(first)
            copy_hT(Turn(0, 1))
            turns(act, turn, turn)

        @block.vector
        def _(dve):
            def norm0_stats(t):
                dve.wait_ge(x_in[t.par], t.dma(1, 1))
                for i in range(TILES):
                    nc.vector.bn_stats(st6[:, 0, i], xin[:, t.par, i]).then_inc(v_st0, 1)
                dve.wait_ge(v_st0, t.count(4, 4))
                nc.vector.memset(spacer[:], 0.0)
                for i in range(TILES):
                    nc.vector.bn_aggr(mv[:, 0, i], st6[:, 0, i]).then_inc(v_mv0, 1)
                dve.wait_ge(v_mv0, t.count(4, 4))
                wait(dve, g_rstd0, t.count(1, 0))
                nc.vector.tensor_scalar(ve[:, 0], mv[:, 0, :, 1], EPS, H_SCALE ** -2, ALU.add,
                                        ALU.mult).then_inc(v_ve0, 1)

            def norm0_shift(t):
                dve.wait_ge(g_rstd0, t.count(1, 1))
                wait(dve, s_h, t.count(4, 0))
                nc.vector.scalar_tensor_tensor(out=nmr[:, 0], in0=mv[:, 0, :, 0], scalar=-1.0, in1=rstd[:, 0],
                                               op0=ALU.mult, op1=ALU.mult).then_inc(v_nmr0, 1)

            def split_hT(t, c):
                dve.wait_ge(s_hT_hi, t.count(3, c + 1))
                nc.vector.tensor_tensor(hT_lo[:, c], ps(J_HT + c), hT_hi[:, c].bitcast(F32),
                                        ALU.subtract).then_inc(v_hT_lo, 1)

            def masks(t):
                adj_f = mask[:, 0:TILES]
                dve.wait_ge(adj_in[t.par], t.dma(1, 1))
                nc.vector.tensor_copy(adj_f, adj_i[:, t.par]).then_inc(v_adj, 1)
                dve.wait_ge(v_adj, t.count(7, 1))
                nc.vector.tensor_scalar(mask[:, TILES:], adj_f, -1.0, 1.0, ALU.mult, ALU.add).then_inc(v_adj, 1)
                nc.vector.tensor_scalar(neg[:, 0:TILES], adj_f, -1.0, BIG, ALU.add, ALU.mult).then_inc(v_adj, 1)
                nc.vector.tensor_scalar(neg[:, TILES:], adj_f, -BIG, None, ALU.mult).then_inc(v_adj, 1)
                nc.vector.tensor_reduce(deg[:, 0], adj_f, AX.X, ALU.add).then_inc(v_adj, 1)
                if isinstance(t.it, int) and t.index == 0:
                    dve.wait_ge(consts_ready, 8)
                for g in range(2):
                    r = slice(g * N, (g + 1) * N)
                    nc.vector.tensor_copy(adj_b[r, t.par, :, P + g * N:P + (g + 1) * N],
                                          mask[r, 0:TILES]).then_inc(v_adj, 1)

            def degrees(t):
                def done(k):
                    dve.wait_ge(v_dcol, t.count(11, k))

                adjT = bank[J_ADJT % 8][:].bitcast(F16)[:, 0:W].rearrange("p (t i) -> p t i", t=TILES)
                dve.wait_ge(adjT_full, t.count(1, 1))
                dve.wait_ge(v_adj, t.count(7, 7))
                nc.vector.tensor_reduce(deg[:, 1], adjT, AX.X, ALU.add).then_inc(v_dcol, 1)
                done(1)
                nc.vector.tensor_scalar(ind[:], deg[:], 1.0, None, ALU.min).then_inc(v_dcol, 1)
                nc.vector.tensor_scalar(degc[:], deg[:], 1.0, None, ALU.max).then_inc(v_dcol, 1)
                done(3)
                nc.vector.tensor_scalar(noedge[:], ind[:, 0], -1.0, 1.0, ALU.mult, ALU.add).then_inc(v_dcol, 1)
                nc.vector.reciprocal(rdeg[:], degc[:]).then_inc(v_dcol, 1)
                for half in range(2):
                    nc.vector.tensor_copy(dcol[:, :, half, 0:2],
                                          deg[:].rearrange("p k t -> p t k")).then_inc(v_dcol, 1)
                    nc.vector.tensor_copy(dcol[:, :, half, 2:4],
                                          ind[:].rearrange("p k t -> p t k")).then_inc(v_dcol, 1)
                done(5)
                nc.vector.tensor_scalar(rdeg_h[:, t.par], rdeg[:], 1.0 / H_SCALE, None, ALU.mult).then_inc(v_dcol, 1)
                nc.vector.tensor_tensor(edges[:], mask[:, 0:TILES],
                                        noedge[:].unsqueeze(2).broadcast_to([P, TILES, N]),
                                        ALU.add).then_inc(v_dcol, 1)

            def residual0(t, i):
                dve.wait_ge(x1_full, t.count(4, i + 1))
                dve.wait_ge(g_xb, t.count(4, i + 1))
                nc.vector.tensor_tensor(x1[:, t.par, i], ps(J_X1[i], D),
                                        x1[:, t.par, i], ALU.add).then_inc(v_x1, 1)
                dve.wait_ge(v_x1, t.count(4, i + 1))
                nc.vector.bn_stats(st6[:, 1, i], x1[:, t.par, i]).then_inc(v_st, 1)
                dve.wait_ge(v_st, t.count(4, i + 1))
                nc.vector.memset(spacer[:], 0.0)
                nc.vector.bn_aggr(mv[:, 1, i], st6[:, 1, i]).then_inc(v_mv, 1)
                dve.wait_ge(v_mv, t.count(4, i + 1))
                nc.vector.tensor_scalar(ve[:, 1, i:i + 1], mv[:, 1, i, 1:2], EPS, H_SCALE ** -2, ALU.add,
                                        ALU.mult).then_inc(v_ve, 1)

            def norm1_shift(t, i):
                dve.wait_ge(g_rstd, t.count(4, i + 1))
                nc.vector.scalar_tensor_tensor(out=nmr[:, 1, i:i + 1], in0=mv[:, 1, i, 0:1], scalar=-1.0,
                                               in1=rstd[:, 1, i:i + 1], op0=ALU.mult, op1=ALU.mult).then_inc(v_nmr, 1)

            def split_h2(t, i):
                dve.wait_ge(s_h2_hi, t.count(4, i + 1))
                nc.vector.tensor_tensor(h2_lo[:, i], h[:, i], h2_hi[:, i], ALU.subtract).then_inc(v_h2_lo, 1)

            def shift_scores(t):
                dve.wait_ge(s_sc, t.count(1, 1))
                nc.vector.tensor_tensor(a[:].rearrange("p (m t) j -> p m t j", m=2),
                                        sc[:].unsqueeze(1).broadcast_to([P, 2, TILES, N]),
                                        mask[:].rearrange("p (m t) j -> p m t j", m=2), ALU.mult).then_inc(v_a, 1)
                dve.wait_ge(v_a, t.count(3, 1))
                nc.vector.tensor_tensor(a[:], a[:], neg[:], ALU.add).then_inc(v_a, 1)
                dve.wait_ge(v_a, t.count(3, 2))
                nc.vector.tensor_reduce(amax[:], a[:], AX.X, ALU.max).then_inc(v_f, 1)
                dve.wait_ge(v_f, t.count(8, 1))
                nc.vector.tensor_tensor(a[:], a[:], amax[:].unsqueeze(2).broadcast_to([P, 2 * TILES, N]),
                                        ALU.subtract).then_inc(v_a, 1)

            def weights(t):
                dve.wait_ge(s_exp, t.count(1, 1))
                nc.vector.tensor_reduce(esum[:], e[:], AX.X, ALU.add).then_inc(v_f, 1)
                dve.wait_ge(v_f, t.count(8, 2))
                nc.vector.reciprocal(rsum[:], esum[:]).then_inc(v_f, 1)
                dve.wait_ge(v_f, t.count(8, 3))
                nc.vector.tensor_tensor(rsd[:], rsum[:, 0:TILES], rdeg[:, 0], ALU.mult).then_inc(v_f, 1)
                dve.wait_ge(v_f, t.count(8, 4))
                nc.vector.tensor_tensor(z[:], e[:, 0:TILES], rsd[:].unsqueeze(2).broadcast_to([P, TILES, N]),
                                        ALU.mult).then_inc(v_f, 1)
                for g in range(2):
                    r = slice(g * N, (g + 1) * N)
                    last = nc.vector.tensor_tensor(An[r, :, r], e[r, TILES:],
                                                   rsum[r, TILES:].unsqueeze(2).broadcast_to([N, TILES, N]),
                                                   ALU.mult)
                last.then_inc(v_An, 1)

            def fusion(t):
                dve.wait_ge(s_zexp, t.count(1, 1))
                nc.vector.tensor_tensor(zm[:], zx[:], edges[:], ALU.mult).then_inc(v_f, 1)
                dve.wait_ge(v_f, t.count(8, 6))
                nc.vector.tensor_reduce(fsum[:], zm[:], AX.X, ALU.add).then_inc(v_f, 1)
                dve.wait_ge(v_f, t.count(8, 7))
                nc.vector.reciprocal(frec[:], fsum[:]).then_inc(v_f, 1)
                dve.wait_ge(v_f, t.count(8, 8))
                for g in range(2):
                    r = slice(g * N, (g + 1) * N)
                    last = nc.vector.tensor_tensor(Fn[r, :, r], zm[r],
                                                   frec[r].unsqueeze(2).broadcast_to([N, TILES, N]), ALU.mult)
                last.then_inc(v_Fn, 1)

            def split_fa(t, job, hi_ready, part, signal):
                dve.wait_ge(hi_ready, t.count(1, 1))
                nc.vector.scalar_tensor_tensor(out=fa_lo[:, :, part], in0=ps(job).rearrange("p (t i) -> p t i", t=TILES),
                                               scalar=F_SCALE, in1=fa_hi[:, :, part], op0=ALU.mult,
                                               op1=ALU.subtract).then_inc(signal, 1)

            def result(t, i):
                result_self(t, i)
                result_adj(t, i)
                result_rev(t, i)

            def result_self(t, i):
                y = x1[:, t.par, i]
                dve.wait_ge(out_full, t.count(12, N_SELF[i]))
                nc.vector.scalar_tensor_tensor(out=y, in0=ps(J_SELF[i], D), scalar=1.0 / H_SCALE, in1=y,
                                               op0=ALU.mult, op1=ALU.add).then_inc(v_out_step, 1)

            def result_adj(t, i):
                y = x1[:, t.par, i]
                dve.wait_ge(out_full, t.count(12, N_ADJ[i]))
                dve.wait_ge(v_out_step, t.count(8, 2 * i + 1))
                nc.vector.scalar_tensor_tensor(out=y, in0=ps(J_ADJ[i], D), scalar=rdeg_h[:, t.par, 0, i:i + 1], in1=y,
                                               op0=ALU.mult, op1=ALU.add).then_inc(v_out_step, 1)

            def result_rev(t, i):
                y = x1[:, t.par, i]
                dve.wait_ge(out_full, t.count(12, N_REV[i]))
                dve.wait_ge(v_out_step, t.count(8, 2 * i + 2))
                nc.vector.scalar_tensor_tensor(out=y, in0=ps(J_REV[i], D), scalar=rdeg_h[:, t.par, 1, i:i + 1], in1=y,
                                               op0=ALU.mult, op1=ALU.add).then_inc(v_out, 1)

            def split_yz(t, k):
                dve.wait_ge(s_yz_hi, t.count(6, k + 1))
                part = slice(2 * (k % 2), 2 * (k % 2) + 2)
                nc.vector.scalar_tensor_tensor(out=yz_lo[:, k // 2, part],
                                               in0=bank[(J_YZ + k) % 8][:].rearrange("p (t i) -> p t i", t=2),
                                               scalar=1.0 / (H_SCALE * F_SCALE), in1=yz_hi[:, k // 2, part].bitcast(F32),
                                               op0=ALU.mult, op1=ALU.subtract).then_inc(v_yz_lo, 1)

            def split_agg(t, k):
                dve.wait_ge(s_agg_hi, t.count(6, k + 1))
                part = slice(2 * (k // C), 2 * (k // C) + 2)
                nc.vector.tensor_tensor(yz_lo[:, k % C, part], bank[J_AGG[k] % 8][:].rearrange("p (t i) -> p t i", t=2),
                                        yz_hi[:, k % C, part].bitcast(F32), ALU.subtract).then_inc(v_agg_lo, 1)

            def split_h2T(t, c):
                dve.wait_ge(s_h2T_hi, t.count(3, c + 1))
                nc.vector.tensor_tensor(hT_lo[:, c], ps(J_H2T + c), hT_hi[:, c].bitcast(F32),
                                        ALU.subtract).then_inc(v_h2T_lo, 1)

            def turn(t):
                n, m = t.plus(1), t.plus(2)
                more, more2 = not is_last(t, 1), not is_last(t, 2)
                for k in range(2 * C):
                    split_yz(t, k)
                if more:
                    masks(n)
                if more2:
                    norm0_stats(m)
                residual0(t, 0)
                norm1_shift(t, 0)
                residual0(t, 1)
                split_h2(t, 0)
                norm1_shift(t, 1)
                if more:
                    degrees(n)
                split_h2(t, 1)
                residual0(t, 2)
                norm1_shift(t, 2)
                residual0(t, 3)
                split_h2(t, 2)
                norm1_shift(t, 3)
                split_h2(t, 3)
                for k in range(C):
                    split_agg(t, k)
                for c in range(C):
                    split_h2T(t, c)
                for k in range(C, 2 * C):
                    split_agg(t, k)
                if more:
                    shift_scores(n)
                if more:
                    weights(n)
                result(t, 0)
                if more:
                    fusion(n)
                if more2:
                    norm0_shift(m)
                result(t, 1)
                result(t, 2)
                if more:
                    split_fa(n, J_FT, s_fT_hi, slice(0, P), v_fT_lo)
                result_self(t, 3)
                result_adj(t, 3)
                if more:
                    split_fa(n, J_AT, s_af_hi, slice(P, 2 * P), v_af_lo)
                if more2:
                    split_hT(m, 0)
                result_rev(t, 3)
                if more2:
                    split_hT(m, 1)
                    split_hT(m, 2)

            first = Turn(0, 0)
            norm0_stats(first)
            norm0_shift(first)
            dve.wait_ge(c_in, 16 * 18)
            dve.wait_ge(consts_ready, 8)
            nc.vector.tensor_copy(b3m[:], b3c[:].unsqueeze(2).broadcast_to([P, C, P])).then_inc(prep_dve, 1)
            for k in range(2):
                nc.vector.tensor_copy(relL[:, k, k:k + LO + 1:LO],
                                      relE[:, k:k + 1].broadcast_to([P, 2])).then_inc(prep_dve, 1)

            def split_weight(name):
                for c in range(C):
                    dve.wait_ge(prep_hi, names.index(name) * C + c + 1)
                    nc.vector.tensor_tensor(w_lo[name][:, c], prep_bank(name, c), w_hi[name][:, c].bitcast(F32),
                                            ALU.subtract).then_inc(prep_lo, 1)

            split_weight("G")
            dve.wait_ge(prep_full, FULL["b1W2"])
            nc.vector.tensor_scalar(tb[:], prep_bank("b1W2", n=C), H_SCALE, None, ALU.mult).then_inc(prep_dve, 1)
            masks(first)
            for c in range(C):
                split_hT(first, c)
            for c in range(C):
                dve.wait_ge(prep_full, FULL["W4T"] + c)
                nc.vector.tensor_copy(W4T[:, c], prep_bank("W4T", c)).then_inc(prep_dve, 1)
            split_weight("W34T")
            nc.vector.tensor_tensor(bias0[:], bias0[:], b4bc[:], ALU.add).then_inc(prep_dve, 1)
            dve.wait_ge(prep_full, FULL["bias"])
            dve.wait_ge(prep_dve, 8)
            nc.vector.tensor_tensor(bias0[:], prep_bank("bias"), bias0[:], ALU.add).then_inc(prep_dve, 1)
            degrees(first)
            split_weight("W3T")
            for k, w in enumerate(("WrT", "WrrT")):
                dve.wait_ge(prep_full, FULL[w])
                nc.vector.tensor_copy(WrTs[:, k], prep_bank(w)).then_inc(prep_dve, 1)
            norm0_stats(Turn(0, 1))
            shift_scores(first)
            split_weight("WadjT")
            weights(first)
            dve.wait_ge(prep_full, FULL["rows"])
            nc.vector.tensor_tensor(rows[:], prep_bank("rows")[0:64], rows_b[:], ALU.add).then_inc(prep_dve, 1)
            dve.wait_ge(prep_dve, 12)
            nc.vector.tensor_scalar(rows[:], rows[:], H_SCALE, None, ALU.mult).then_inc(prep_dve, 1)
            dve.wait_ge(prep_dve, 13)
            nc.vector.tensor_copy(rows_r[:], rows[:]).then_inc(prep_dve, 1)
            nc.vector.tensor_copy(rank[0:LO], rows[0:LO]).then_inc(prep_dve, 1)
            dve.wait_ge(prep_dve, 14)
            nc.vector.tensor_tensor(rank[LO:64], rows[LO:64], rows_r[LO:64].bitcast(F32),
                                    ALU.subtract).then_inc(prep_dve, 1)
            norm0_shift(Turn(0, 1))
            split_weight("WrevT")
            fusion(first)
            split_weight("WselfT")
            split_fa(first, J_FT, s_fT_hi, slice(0, P), v_fT_lo)
            split_fa(first, J_AT, s_af_hi, slice(P, 2 * P), v_af_lo)
            for c in range(C):
                split_hT(Turn(0, 1), c)
            turns(dve, turn, turn)

        @block.tensor
        def _(pe):
            def chunk(c):
                return slice(c * P, (c + 1) * P)

            def group(to, products):
                for k, (lhsT, rhs) in enumerate(products):
                    last = nc.tensor.matmul(to, lhsT, rhs, start=(k == 0), stop=(k == len(products) - 1))
                return last

            def three(l_hi, l_lo, r_hi, r_lo):
                return [(l_hi, r_hi), (l_hi, r_lo), (l_lo, r_hi)]

            def hT_job(t):
                pe.wait_ge(s_h, t.count(4, 4))
                for c in range(C):
                    for i in range(TILES):
                        last = nc.tensor.transpose(ps(J_HT + c)[:, chunk(i)], h[:, i, chunk(c)], id32[:])
                    last.then_inc(hT_full, 1)

            def t_job(t, c):
                if c == 0:
                    pe.wait_ge(v_hT_lo, t.count(3, 3))
                g = [three(w_hi["G"][:, d, chunk(c)], w_lo["G"][:, d, chunk(c)], hT_hi[:, d], hT_lo[:, d])
                     for d in range(C)]
                group(ps(J_T[c]), sum(g, [])).then_inc(t_full, 1)

            def adjT_job(t):
                pe.wait_ge(v_adj, t.count(7, 7))
                to = bank[J_ADJT % 8][:].bitcast(F16)
                for i in range(TILES):
                    last = nc.tensor.transpose(to[:, chunk(i)], adj_b[:, t.par, i, P:2 * P], id16[:])
                last.then_inc(adjT_full, 1)

            def drow_job(t):
                pe.wait_ge(v_dcol, t.count(11, 11))
                pe.wait_ge(s_adjT, t.count(1, 1))
                to = bank[J_ADJT % 8][:].bitcast(F16)
                for i in range(TILES):
                    last = nc.tensor.transpose(to[:, W + i * P:W + (i + 1) * P],
                                               dcol[:, i].rearrange("p a b -> p (a b)"), id16[:])
                last.then_inc(drow_full, 1)

            def att_job(t):
                pe.wait_ge(s_tT, t.count(3, 3))
                pe.wait_ge(g_hT, t.count(3, 3))
                for i in range(TILES):
                    last = group(ps(J_ATT)[:, chunk(i)], [(tT[:, c, chunk(i)], hT[:, c, chunk(i)]) for c in range(C)])
                last.then_inc(att_full, 1)

            def fT_job(t):
                pe.wait_ge(v_Fn, t.count(1, 1))
                for i in range(TILES):
                    last = nc.tensor.transpose(ps(J_FT)[:, chunk(i)], Fn[:, i], id32[:])
                last.then_inc(fT_full, 1)
                for i in range(TILES):
                    last = nc.tensor.transpose(ps(J_AT)[:, chunk(i)], An[:, i], id32[:])
                last.then_inc(aT_full, 1)

            def af_job(t):
                pe.wait_ge(s_AT, t.count(1, 1))
                for i in range(TILES):
                    last = group(ps(J_AT)[:, chunk(i)], [(Fn[:, i], AT[:, i])])
                last.then_inc(af_full, 1)

            def x1_job(t, i):
                y, zz = slice(0, P), slice(P, 2 * P)
                g = [three(yz_hi[:, c, i, part], yz_lo[:, c, i, part], w_hi[w][:, c], w_lo[w][:, c])
                     for w, part in (("W3T", y), ("W34T", zz)) for c in range(C)]
                group(ps(J_X1[i], D), sum(g, [])).then_inc(x1_full, 1)

            def self_job(t, i):
                g = [three(hT_hi[:, c, chunk(i)], hT_lo[:, c, chunk(i)], w_hi["WselfT"][:, c], w_lo["WselfT"][:, c])
                     for c in range(C)]
                group(ps(J_SELF[i], D), sum(g, [(drow[:, t.par, chunk(i)], rank[:])])).then_inc(out_full, 1)

            def neighbours_job(i, job, part, w):
                g = [three(yz_hi[:, c, i, part], yz_lo[:, c, i, part], w_hi[w][:, c], w_lo[w][:, c]) for c in range(C)]
                group(ps(job, D), sum(g, [])).then_inc(out_full, 1)

            def adj_job(i):
                neighbours_job(i, J_ADJ[i], slice(0, P), "WadjT")

            def rev_job(i):
                neighbours_job(i, J_REV[i], slice(P, 2 * P), "WrevT")

            def yz_job(t, k):
                for half in range(2):
                    i, c = 2 * (k % 2) + half, k // 2
                    last = group(ps(J_YZ + k)[:, half * 2 * P:(half + 1) * 2 * P],
                                 three(h_hi[:, t.par, i, chunk(c)], h_lo[:, t.par, i, chunk(c)],
                                       fa_hi[:, i], fa_lo[:, i]))
                last.then_inc(yz_full, 1)

            def agg_job(t, k):
                for half in range(2):
                    i, c = 2 * (k // C) + half, k % C
                    last = group(ps(J_AGG[k])[:, half * 2 * P:(half + 1) * 2 * P],
                                 [(h2_hi[:, i, chunk(c)], adj_b[:, t.par, i]),
                                  (h2_lo[:, i, chunk(c)], adj_b[:, t.par, i])])
                last.then_inc(agg_full, 1)

            def turn(t):
                n, m = t.plus(1), t.plus(2)
                more, more2 = not is_last(t, 1), not is_last(t, 2)
                pe.wait_ge(v_fT_lo, t.count(1, 1))
                pe.wait_ge(v_af_lo, t.count(1, 1))
                pe.wait_ge(g_h_lo, t.count(4, 4))
                for k in range(2 * C):
                    if k == 2:
                        wait(pe, v_out, t.count(4, 0))
                    if k >= 4 and more:
                        pe.wait_ge(v_hT_lo, n.count(3, k - 3))
                    yz_job(t, k)
                if more:
                    t_job(n, 0)
                    t_job(n, 1)
                pe.wait_ge(v_yz_lo, t.count(6, 6))
                x1_job(t, 0)
                x1_job(t, 1)
                if more:
                    adjT_job(n)
                x1_job(t, 2)
                x1_job(t, 3)
                if more:
                    t_job(n, 2)
                    drow_job(n)
                pe.wait_ge(s_adjT, t.count(1, 1))
                pe.wait_ge(v_h2_lo, t.count(4, 2))
                for k in range(C):
                    agg_job(t, k)
                if more:
                    att_job(n)
                if more:
                    pe.wait_ge(s_drow, n.count(1, 1))
                pe.wait_ge(v_x1, t.count(4, 3))
                for i in range(TILES):
                    pe.wait_ge(s_h2, t.count(4, i + 1))
                    for c in range(C):
                        last = nc.tensor.transpose(ps(J_H2T + c)[:, chunk(i)], h[:, i, chunk(c)], id32[:])
                        if i == TILES - 1:
                            last.then_inc(h2T_full, 1)
                pe.wait_ge(v_h2_lo, t.count(4, 4))
                for k in range(C, 2 * C):
                    if k == 4 and more:
                        pe.wait_ge(s_sc, n.count(1, 1))
                    if k == 5:
                        pe.wait_ge(v_agg_lo, t.count(6, 1))
                    agg_job(t, k)
                pe.wait_ge(v_agg_lo, t.count(6, 3))
                adj_job(0)
                rev_job(0)
                pe.wait_ge(s_drow, t.count(1, 1))
                pe.wait_ge(v_h2T_lo, t.count(3, 3))
                self_job(t, 0)
                self_job(t, 1)
                adj_job(1)
                pe.wait_ge(v_agg_lo, t.count(6, 6))
                rev_job(1)
                self_job(t, 2)
                adj_job(2)
                pe.wait_ge(v_out, t.count(4, 1))
                rev_job(2)
                if more:
                    fT_job(n)
                pe.wait_ge(v_out, t.count(4, 2))
                self_job(t, 3)
                adj_job(3)
                if more:
                    af_job(n)
                pe.wait_ge(v_out, t.count(4, 3))
                if more2:
                    hT_job(m)
                rev_job(3)

            def transposed(name, natural_w):
                for c in range(C):
                    for o in range(C):
                        last = nc.tensor.transpose(prep_bank(name, c)[:, chunk(o)], natural_w[:, o, chunk(c)], id32[:])
                    last.then_inc(prep_full, 1)

            first = Turn(0, 0)
            pe.wait_ge(ident_ready, 2)
            pe.wait_ge(w_in[0], 32)
            for c in range(C):
                group(prep_bank("G", c), [(W1n[:, o, chunk(c)], W2n[:, o]) for o in range(C)]).then_inc(prep_full, 1)
            pe.wait_ge(c_in, 16 * 18)
            for c in range(C):
                last = group(prep_bank("b1W2", n=C)[:, c:c + 1],
                             [(W2n[:, o, chunk(c)], b1c[:, o:o + 1]) for o in range(C)])
            last.then_inc(prep_full, 1)
            hT_job(first)
            pe.wait_ge(w_in[1], 32)
            pe.wait_ge(prep_lo, 3)
            pe.wait_ge(prep_dve, 4)
            transposed("W4T", W4n)
            for c in range(C):
                t_job(first, c)
            pe.wait_ge(prep_dve, 7)
            for c in range(C):
                group(prep_bank("W34T", c), [(W3n[:, o, chunk(c)], W4T[:, o]) for o in range(C)]).then_inc(prep_full, 1)
            group(prep_bank("bias"), [(b3m[:, o], W4T[:, o]) for o in range(C)]).then_inc(prep_full, 1)
            adjT_job(first)
            pe.wait_ge(s_tT, 2)
            pe.wait_ge(prep_lo, 6)
            transposed("W3T", W3n)
            for k, w in enumerate(("WrT", "WrrT")):
                for o in range(C):
                    last = nc.tensor.transpose(prep_bank(w)[:, chunk(o)], WrN[:, k, o], id32[:])
                last.then_inc(prep_full, 1)
            drow_job(first)
            att_job(first)
            pe.wait_ge(w_in[2], 16)
            pe.wait_ge(prep_dve, 9)
            pe.wait_ge(prep_lo, 9)
            transposed("WadjT", W1n)
            pe.wait_ge(prep_dve, 11)
            group(prep_bank("rows")[0:64], [(relL[:, k], WrTs[:, k]) for k in range(2)]).then_inc(prep_full, 1)
            pe.wait_ge(w_in[3], 16)
            pe.wait_ge(s_drow, 1)
            transposed("WrevT", W2n)
            pe.wait_ge(w_in[4], 16)
            pe.wait_ge(prep_lo, 12)
            transposed("WselfT", W3n)
            pe.wait_ge(prep_dve, 16)
            pe.wait_ge(prep_lo, 15)
            fT_job(first)
            af_job(first)
            pe.wait_ge(prep_lo, 18)
            hT_job(Turn(0, 1))
            turns(pe, turn, turn)


INPUTS = ("x", "adj", "L0_gnn_W1", "L0_gnn_b1", "L0_gnn_W2", "L0_gnn_b2", "L0_gnn_W3", "L0_gnn_b3", "L0_gnn_W4",
          "L0_gnn_b4", "L1_gnn_E", "L1_gnn_Wadj", "L1_gnn_badj", "L1_gnn_Wrev", "L1_gnn_brev", "L1_gnn_Wself",
          "L1_gnn_bself", "L1_gnn_Wr", "L1_gnn_br", "L1_gnn_Wrr", "L1_gnn_brr")


def kernel(**inputs):
    import numpy as np
    import concourse.bacc as bacc
    from concourse.bass_utils import run_bass_kernel_spmd

    nc = bacc.Bacc("TRN2", target_bir_lowering=False, num_devices=1)
    arrays, d = {}, {}
    for name in INPUTS:
        v = np.ascontiguousarray(inputs[name])
        arrays[f"in_{name}"] = v
        d[name] = nc.dram_tensor(f"in_{name}", v.shape, mybir.dt.from_np(v.dtype), kind="ExternalInput").ap()
    out = nc.dram_tensor("out", (GRAPHS, N, D), F32, kind="ExternalOutput").ap()
    a, b = "L0_gnn_", "L1_gnn_"
    build(nc, d["x"], d["adj"], [d[a + w] for w in ("W1", "W2", "W3", "W4")],
          [d[a + w] for w in ("b1", "b2", "b3", "b4")], d[b + "E"],
          [d[b + w] for w in ("Wadj", "Wrev", "Wself")], [d[b + w] for w in ("badj", "brev", "bself")],
          d[b + "Wr"], d[b + "br"], d[b + "Wrr"], d[b + "brr"], out)
    r = run_bass_kernel_spmd(nc, [arrays], core_ids=[0])
    return r.results[0]["out"]
```

```python
from contextlib import ExitStack

import concourse.bass as bass
from concourse import mybir

F32 = mybir.dt.float32
F32R = mybir.dt.float32r
F16 = mybir.dt.float16
I32 = mybir.dt.int32
ALU = mybir.AluOpType
ACT = mybir.ActivationFunctionType
AX = mybir.AxisListType

P = 128
GRAPHS, N, D = 128, 64, 384
TILES = 4
W = TILES * P
ST = GRAPHS * N // W
C = D // P
R = 128
REL, REL_REV = 1, 41
EPS = 1e-5
H_SCALE = 64.0
F_SCALE = 1024.0
ATT_SCALE = 1.0 / (28.0 * H_SCALE * H_SCALE)
BIG = 1e9 / ATT_SCALE
LO = 32

J_YZ = 0
J_T = (6, 7, 13)
J_X1 = (8, 9, 11, 12)
J_ADJT = 10
J_ATT = 13
J_AGG = (14, 15, 16, 20, 21, 22)
J_H2T = 17
J_SELF, J_ADJ, J_REV = (25, 26, 29, 34), (23, 27, 30, 35), (24, 28, 31, 39)
J_FT, J_AT = 32, 33
J_HT = 36
N_SELF, N_ADJ, N_REV = (3, 4, 7, 10), (1, 5, 8, 11), (2, 6, 9, 12)


class Turn:

    def __init__(self, it, u):
        self.it, self.u = it, u

    def plus(self, n):
        return Turn(self.it, self.u + n)

    @property
    def par(self):
        return self.u % 2

    @property
    def index(self):
        return self.it * 2 + self.u

    def count(self, per, k):
        return self.it * (2 * per) + (self.u * per + k)

    def dma(self, per, k):
        return (self.it + self.u // 2) * (16 * per) + 16 * k


def wait(eng, sem, value):
    if isinstance(value, int) and value <= 0:
        return
    eng.wait_ge(sem, value)


def build(nc, x, adj, w0, b0, E, w1, b1, Wr, br, Wrr, brr, out):
    W1, W2, W3, W4 = w0
    Wadj, Wrev, Wself = w1

    x_v = x.rearrange("(s t h) n d -> s (h n) t d", t=TILES, h=2)
    out_v = out.rearrange("(s t h) n d -> s (h n) t d", t=TILES, h=2)
    adj_v = adj.rearrange("(s t h) i j -> s (h i) t j", t=TILES, h=2)

    with ExitStack() as ctx:
        def sb(name, shape, dt=F32):
            return ctx.enter_context(nc.sbuf_tensor(name, shape, dt))

        def sem(name):
            return ctx.enter_context(nc.semaphore(name))

        bank = [ctx.enter_context(nc.psum_tensor(f"bank{i}", [P, 512], F32)) for i in range(8)]

        def ps(job, n=512):
            return bank[job % 8][:, 0:n]

        names = ("G", "W34T", "W3T", "WadjT", "WrevT", "WselfT")
        w_hi = {k: sb(k + "_hi", [P, C, D], F32R) for k in names}
        w_lo = {k: sb(k + "_lo", [P, C, D], F32R) for k in names}
        W4T = sb("W4T", [P, C, D])
        relE = sb("relE", [P, 2])
        relL = sb("relL", [P, 2, 64])
        b1c = sb("b1c", [P, C])
        b3c = sb("b3c", [P, C])
        b3m = sb("b3m", [P, C, P])
        tb = sb("tb", [P, C])
        bias0 = sb("bias0", [P, D])
        b4bc = sb("b4bc", [P, D])
        rows = sb("rows", [64, D])
        rows_b = sb("rows_b", [64, D])
        rows_r = sb("rows_r", [64, D], F32R)
        rank = sb("rank", [64, D], F32R)
        id32 = sb("id32", [P, P])
        id16 = sb("id16", [P, P], F16)
        minus_half = sb("minus_half", [P, TILES])

        xin = sb("xin", [P, 2, TILES, D])
        x1 = sb("x1", [P, 2, TILES, D])
        h = sb("h", [P, TILES, D])
        h_parts = sb("h_parts", [P, 2, TILES, 2, D], F16)
        h2_parts = sb("h2_parts", [P, TILES, 2, D], F16)
        hT = sb("hT", [P, C, W])
        hT_hi = sb("hT_hi", [P, C, W], F32R)
        hT_lo = sb("hT_lo", [P, C, W], F32R)
        tT = sb("tT", [P, C, W])
        yz_hi = sb("yz_hi", [P, C, TILES, 2 * P], F32R)
        yz_lo = sb("yz_lo", [P, C, TILES, 2 * P], F32R)
        st6 = sb("st6", [P, 2, TILES, 6])
        mv = sb("mv", [P, 2, TILES, 2])
        ve = sb("ve", [P, 2, TILES])
        rstd = sb("rstd", [P, 2, TILES])
        nmr = sb("nmr", [P, 2, TILES])
        spacer = sb("spacer", [P, 1])
        adj_i = sb("adj_i", [P, 2, TILES, N], I32)
        mask = sb("mask", [P, 2 * TILES, N])
        neg = sb("neg", [P, 2 * TILES, N])
        edges = sb("edges", [P, TILES, N])
        adj_b = sb("adj_b", [P, 2, TILES, 2 * P], F16)
        deg = sb("deg", [P, 2, TILES])
        ind = sb("ind", [P, 2, TILES])
        noedge = sb("noedge", [P, TILES])
        degc = sb("degc", [P, 2, TILES])
        rdeg = sb("rdeg", [P, 2, TILES])
        rdeg_h = sb("rdeg_h", [P, 2, 2, TILES])
        dcol = sb("dcol", [P, TILES, 4, 32], F16)
        drow = sb("drow", [64, 2, W], F32R)
        sc = sb("sc", [P, TILES, N])
        a = sb("a", [P, 2 * TILES, N])
        e = sb("e", [P, 2 * TILES, N])
        amax = sb("amax", [P, 2 * TILES])
        esum = sb("esum", [P, 2 * TILES])
        rsum = sb("rsum", [P, 2 * TILES])
        rsd = sb("rsd", [P, TILES])
        z = sb("z", [P, TILES, N])
        zx = sb("zx", [P, TILES, N])
        zm = sb("zm", [P, TILES, N])
        fsum = sb("fsum", [P, TILES])
        frec = sb("frec", [P, TILES])
        Fn = sb("Fn", [P, TILES, P])
        An = sb("An", [P, TILES, P])
        AT = sb("AT", [P, TILES, P])
        fa_hi = sb("fa_hi", [P, TILES, 2 * P], F16)
        fa_lo = sb("fa_lo", [P, TILES, 2 * P], F16)

        def staged(flat, k):
            return flat[:, k * C * D:(k + 1) * C * D].rearrange("p (c d) -> p c d", c=C)

        x1_flat = x1[:].rearrange("p a t d -> p (a t d)")
        W1n, W2n = staged(x1_flat, 0), staged(x1_flat, 1)
        W3n = sb("W3n", [P, C, D])
        W4n = staged(xin[:, 1].rearrange("p t d -> p (t d)"), 0)
        WrTs = x1_flat[:, 2 * C * D:2 * C * D + 2 * D].rearrange("p (k d) -> p k d", k=2)
        WrN = h2_parts[:].rearrange("p t g d -> p (t g d)").bitcast(F32)[:, 0:2 * D].rearrange("p (k c r) -> p k c r", k=2, c=C)

        x_in = [sem("x_in0"), sem("x_in1")]
        adj_in = [sem("adj_in0"), sem("adj_in1")]
        out_sent = [sem("out_sent0"), sem("out_sent1")]
        w12_in = [sem(f"w12_in{c}") for c in range(C)]
        w_in = {k: sem(k + "_in") for k in ("W4", "W3", "Wadj", "Wrev", "Wself")}
        c_in, r_in = sem("c_in"), sem("r_in")
        ident_ready, consts_ready, zeros_ready = sem("ident_ready"), sem("consts_ready"), sem("zeros_ready")
        prep_dve, prep_full, prep_hi, prep_lo = sem("prep_dve"), sem("prep_full"), sem("prep_hi"), sem("prep_lo")
        yz_full = sem("yz_full")
        hT_full = sem("hT_full")
        t_full = sem("t_full")
        x1_full = sem("x1_full")
        adjT_full = sem("adjT_full")
        drow_full = sem("drow_full")
        att_full = sem("att_full")
        h2T_full = sem("h2T_full")
        agg_full = sem("agg_full")
        out_full = sem("out_full")
        fT_full = sem("fT_full")
        aT_full = sem("aT_full")
        af_full = sem("af_full")
        s_yz_hi = sem("s_yz_hi")
        s_hT_hi = sem("s_hT_hi")
        s_tT = sem("s_tT")
        s_h2 = sem("s_h2")
        s_h2_hi = sem("s_h2_hi")
        s_adjT = sem("s_adjT")
        s_drow = sem("s_drow")
        s_h2T_hi = sem("s_h2T_hi")
        s_agg_hi = sem("s_agg_hi")
        s_sc = sem("s_sc")
        s_exp = sem("s_exp")
        s_zexp = sem("s_zexp")
        s_h = sem("s_h")
        s_h_hi = sem("s_h_hi")
        h_lo_placed = sem("h_lo_placed")
        s_fT_hi = sem("s_fT_hi")
        s_AT = sem("s_AT")
        s_af_hi = sem("s_af_hi")
        v_yz_lo = sem("v_yz_lo")
        v_hT_lo = sem("v_hT_lo")
        v_x1 = sem("v_x1")
        v_st = sem("v_st")
        v_mv = sem("v_mv")
        v_ve = sem("v_ve")
        v_nmr = sem("v_nmr")
        v_h2_lo = sem("v_h2_lo")
        v_h2T_lo = sem("v_h2T_lo")
        v_agg_lo = sem("v_agg_lo")
        v_adj = sem("v_adj")
        v_dcol = sem("v_dcol")
        v_a = sem("v_a")
        v_f = sem("v_f")
        v_An = sem("v_An")
        v_Fn = sem("v_Fn")
        v_st0 = sem("v_st0")
        v_mv0 = sem("v_mv0")
        v_ve0 = sem("v_ve0")
        v_nmr0 = sem("v_nmr0")
        v_fT_lo = sem("v_fT_lo")
        v_af_lo = sem("v_af_lo")
        v_out_step = sem("v_out_step")
        v_out = sem("v_out")
        g_xb = sem("g_xb")
        g_rstd = sem("g_rstd")
        g_rstd0 = sem("g_rstd0")
        g_h_lo = sem("g_h_lo")
        g_hT = sem("g_hT")

        FULL = {"G": 1, "W4T": 4, "b1W2": 7, "bias": 8, "W34T": 9, "W3T": 12, "WrT": 15, "WrrT": 16,
                "WadjT": 17, "WrevT": 20, "rows": 23, "WselfT": 24}

        PREP_BANK = {"G": (0, 1, 2), "W4T": (3, 6, 7), "b1W2": (4,), "bias": (4,), "W34T": (0, 1, 3),
                     "W3T": (2, 5, 6), "WrT": (7,), "WrrT": (4,), "WadjT": (0, 1, 3), "rows": (5,),
                     "WrevT": (2, 6, 7), "WselfT": (3, 4, 5)}

        def prep_bank(name, c=0, n=D):
            return bank[PREP_BANK[name][c]][:, 0:n]

        block = ctx.enter_context(nc.Block())

        def turns(eng, body, last):
            body(Turn(0, 0))
            body(Turn(0, 1))
            with eng.Fori(1, ST // 2 - 1) as it:
                body(Turn(it, 0))
                body(Turn(it, 1))
            body(Turn(ST // 2 - 1, 0))
            last(Turn(ST // 2 - 1, 1))

        def graph(g):
            return slice(g * N, (g + 1) * N)

        def is_last(t, ahead):
            return isinstance(t.it, int) and t.index + ahead >= ST

        @block.sync
        def _(sp):
            def load(t):
                sp.dma_start(xin[:, t.par], x_v[t.index]).then_inc(x_in[t.par], 16)

            def load_adj(t):
                sp.dma_start(adj_i[:, t.par], adj_v[t.index]).then_inc(adj_in[t.par], 16)

            def row(v):
                return v.rearrange("(a d) -> a d", a=1)

            def natural(w):
                return w.rearrange("(c p) d -> p c d", p=P)

            for c in range(C):
                for to, w in ((W1n, W1), (W2n, W2)):
                    sp.dma_start(to[:, c], w[c * P:(c + 1) * P]).then_inc(w12_in[c], 16)
                if c == 0:
                    load(Turn(0, 0))
            sp.dma_start(W4n, natural(W4)).then_inc(w_in["W4"], 16)
            for k in range(2):
                sp.dma_start(relE[:, k:k + 1], E[(REL, REL_REV)[k]].rearrange("(r a) -> r a", a=1),
                             allow_slow_non_contiguous=True).then_inc(c_in, 16)
            for to, v in ((b1c, b0[0]), (b3c, b0[2])):
                sp.dma_start(to[:], v.rearrange("(c p) -> p c", p=P), allow_slow_non_contiguous=True).then_inc(c_in, 16)
            for to, v in ((bias0, b0[2]), (b4bc, b0[3])):
                sp.dma_start(to[:], row(v).broadcast_to([P, D])).then_inc(c_in, 16)
            sp.dma_start(W3n[:], natural(W3)).then_inc(w_in["W3"], 16)
            load_adj(Turn(0, 0))
            load_adj(Turn(0, 1))
            for k, w in enumerate((Wr, Wrr)):
                sp.dma_start(WrN[:, k], w.rearrange("(c p) r -> p c r", p=P)).then_inc(r_in, 16)
            sp.wait_ge(consts_ready, 3)
            for part in (0, LO):
                for k, v in enumerate((br, brr, b1[0], b1[1], b1[2])):
                    sp.dma_start(rows_b[part + k:part + k + 1, :], row(v)).then_inc(r_in, 16)
            sp.wait_ge(prep_full, FULL["G"] + 2)
            sp.dma_start(W1n, natural(Wadj)).then_inc(w_in["Wadj"], 16)
            sp.wait_ge(prep_full, FULL["W4T"] + 2)
            load(Turn(0, 1))
            sp.wait_ge(prep_full, FULL["b1W2"])
            sp.dma_start(W2n, natural(Wrev)).then_inc(w_in["Wrev"], 16)
            sp.wait_ge(prep_full, FULL["W3T"] + 2)
            sp.dma_start(W3n[:], natural(Wself)).then_inc(w_in["Wself"], 16)

            def turn(t):
                if not is_last(t, 2):
                    sp.wait_ge(g_xb, t.count(4, 4))
                    load(t.plus(2))
                    sp.wait_ge(v_adj, t.count(10, 1))
                    load_adj(t.plus(2))
                for i in range(TILES):
                    wait(sp, v_out, t.count(4, i + 1))
                    sp.dma_start(out_v[t.index][:, i], x1[:, t.par, i]).then_inc(out_sent[t.par], 16)

            turns(sp, turn, turn)
            for par in range(2):
                sp.wait_ge(out_sent[par], 16 * TILES * ST // 2)

        @block.gpsimd
        def _(pool):
            nc.gpsimd.memset(id32[:], 0.0).then_inc(zeros_ready, 1)
            nc.gpsimd.memset(id16[:], 0.0).then_inc(zeros_ready, 1)
            pool.wait_ge(zeros_ready, 2)
            for m in (id32, id16):
                nc.gpsimd.affine_select(out=m[:], in_=m[:], compare_op=ALU.not_equal, fill=1.0, base=0,
                                        pattern=[[-1, P]], channel_multiplier=1).then_inc(ident_ready, 1)
            nc.gpsimd.memset(minus_half[:], -0.5).then_inc(consts_ready, 1)
            nc.gpsimd.memset(relL[:], 0.0).then_inc(consts_ready, 1)
            nc.gpsimd.memset(rows_b[:], 0.0).then_inc(consts_ready, 1)
            nc.gpsimd.memset(An[:], 0.0).then_inc(consts_ready, 1)
            nc.gpsimd.memset(dcol[:], 0.0).then_inc(consts_ready, 1)
            pool.wait_ge(consts_ready, 5)
            nc.gpsimd.memset(dcol[:, :, 0:2, 4], 1.0).then_inc(consts_ready, 1)

            def rstd_of(t, ready, signal, ln, part):
                pool.wait_ge(*ready)
                nc.gpsimd.tensor_tensor(rstd[:, ln, part], ve[:, ln, part], minus_half[:, part],
                                        ALU.pow).then_inc(signal, 1)

            def norm0(t):
                wait(pool, s_h_hi, t.count(2, 0))
                rstd_of(t, (v_ve0, t.count(1, 1)), g_rstd0, 0, slice(0, TILES))

            def low_h(t):
                pool.wait_ge(s_h_hi, t.count(2, 2))
                pool.wait_ge(hT_full, t.count(3, 3))
                for g in range(2):
                    nc.gpsimd.tensor_tensor(h[graph(g)], h[graph(g)], h_parts[graph(g), t.par, :, g],
                                            ALU.subtract).then_inc(g_h_lo, 1)
                    pool.wait_ge(g_h_lo, t.count(2, g - 1))

            def add_bias(t):
                wait(pool, out_sent[t.par], t.dma(4, 0))
                pool.wait_ge(x_in[t.par], t.dma(1, 1))
                for i in range(TILES):
                    nc.gpsimd.tensor_tensor(x1[:, t.par, i], xin[:, t.par, i], bias0[:], ALU.add).then_inc(g_xb, 1)

            def join_hT(t):
                for c in range(C):
                    pool.wait_ge(v_hT_lo, t.count(3, c + 1))
                    wait(pool, att_full, t.count(1, 0))
                    nc.gpsimd.tensor_tensor(hT[:, c], hT_hi[:, c].bitcast(F32), hT_lo[:, c].bitcast(F32),
                                            ALU.add).then_inc(g_hT, 1)

            def turn(t):
                if not is_last(t, 1):
                    low_h(t.plus(1))
                    join_hT(t.plus(1))
                for i in range(TILES):
                    rstd_of(t, (v_ve, t.count(4, i + 1)), g_rstd, 1, slice(i, i + 1))
                if not is_last(t, 2):
                    norm0(t.plus(2))
                if not is_last(t, 1):
                    add_bias(t.plus(1))

            pool.wait_ge(consts_ready, 1)
            norm0(Turn(0, 0))
            join_hT(Turn(0, 0))
            norm0(Turn(0, 1))
            pool.wait_ge(prep_full, FULL["rows"])
            pool.wait_ge(prep_dve, 9)
            add_bias(Turn(0, 0))
            turns(pool, turn, turn)

        @block.scalar
        def _(act):
            def norm0(t):
                act.wait_ge(x_in[t.par], t.dma(1, 1))
                act.wait_ge(v_nmr0, t.count(1, 1))
                wait(act, v_h2_lo, t.count(8, -8))
                wait(act, h_lo_placed, t.count(2, 0))
                for i in range(TILES):
                    nc.scalar.activation(h[:, i], xin[:, t.par, i], ACT.Relu, bias=nmr[:, 0, i:i + 1],
                                         scale=rstd[:, 0, i:i + 1]).then_inc(s_h, 1)

            def high_h(t, g):
                act.wait_ge(s_h, t.count(4, 4))
                nc.scalar.activation(h_parts[graph(g), t.par, :, g], h[graph(g)], ACT.Copy).then_inc(s_h_hi, 1)

            def place_low_h(t):
                act.wait_ge(g_h_lo, t.count(2, 0))
                for g in range(2):
                    nc.scalar.activation(h_parts[graph(1 - g), t.par, :, g], h[graph(g)], ACT.Copy).then_inc(h_lo_placed, 1)

            def copy_hT(t):
                for c in range(C):
                    act.wait_ge(hT_full, t.count(3, c + 1))
                    nc.scalar.activation(hT_hi[:, c], ps(J_HT + c), ACT.Copy).then_inc(s_hT_hi, 1)

            def copy_tT(t, c):
                act.wait_ge(t_full, t.count(3, c + 1))
                nc.scalar.activation(tT[:, c], ps(J_T[c]), ACT.Identity,
                                     bias=tb[:, c:c + 1]).then_inc(s_tT, 1)

            def copy_adjT(t):
                act.wait_ge(v_dcol, t.count(11, 1))
                nc.scalar.activation(adj_b[:, t.par, :, 0:P],
                                     bank[J_ADJT % 8][:].bitcast(F16)[:, 0:W].rearrange("p (t i) -> p t i", t=TILES),
                                     ACT.Copy).then_inc(s_adjT, 1)

            def copy_drow(t):
                act.wait_ge(drow_full, t.count(1, 1))
                nc.scalar.activation(drow[:, t.par], bank[J_ADJT % 8][0:64].bitcast(F16)[:, W:2 * W],
                                     ACT.Copy).then_inc(s_drow, 1)

            def norm1(t, i):
                act.wait_ge(v_nmr, t.count(4, i + 1))
                if i == 0 and not is_last(t, 1):
                    wait(act, h_lo_placed, t.plus(1).count(2, 2))
                nc.scalar.activation(h[:, i], x1[:, t.par, i], ACT.Relu, bias=nmr[:, 1, i:i + 1],
                                     scale=rstd[:, 1, i:i + 1]).then_inc(s_h2, 1)
                act.wait_ge(s_h2, t.count(4, i + 1))
                for g in range(2):
                    nc.scalar.activation(h2_parts[graph(g), i, g], h[graph(g), i], ACT.Copy).then_inc(s_h2_hi, 1)

            def copy_scores(t):
                act.wait_ge(att_full, t.count(1, 1))
                for g in range(2):
                    r = slice(g * N, (g + 1) * N)
                    last = nc.scalar.activation(sc[r], bank[J_ATT % 8][r].rearrange("p (t j) -> p t j", t=TILES)[:, :, r],
                                                ACT.Copy)
                last.then_inc(s_sc, 1)

            def exp_scores(t):
                act.wait_ge(v_a, t.count(3, 3))
                nc.scalar.activation(e[:], a[:], ACT.Exp, scale=ATT_SCALE).then_inc(s_exp, 1)

            def exp_fusion(t):
                act.wait_ge(v_f, t.count(8, 5))
                nc.scalar.activation(zx[:], z[:], ACT.Exp).then_inc(s_zexp, 1)

            def copy_fT(t):
                act.wait_ge(fT_full, t.count(1, 1))
                nc.scalar.activation(fa_hi[:, :, 0:P], ps(J_FT).rearrange("p (t i) -> p t i", t=TILES),
                                     ACT.Copy, scale=F_SCALE).then_inc(s_fT_hi, 1)
                act.wait_ge(aT_full, t.count(1, 1))
                nc.scalar.activation(AT[:], ps(J_AT).rearrange("p (t i) -> p t i", t=TILES),
                                     ACT.Copy).then_inc(s_AT, 1)

            def copy_af(t):
                act.wait_ge(af_full, t.count(1, 1))
                nc.scalar.activation(fa_hi[:, :, P:2 * P], ps(J_AT).rearrange("p (t i) -> p t i", t=TILES),
                                     ACT.Copy, scale=F_SCALE).then_inc(s_af_hi, 1)

            def pair(job):
                return bank[job % 8][:].rearrange("p (t i) -> p t i", t=2)

            def turn(t):
                n = t.plus(1)
                more, more2 = not is_last(t, 1), not is_last(t, 2)
                for k in range(2 * C):
                    act.wait_ge(yz_full, t.count(6, k + 1))
                    nc.scalar.activation(yz_hi[:, k % C, 2 * (k // C):2 * (k // C) + 2], pair(J_YZ + k), ACT.Copy,
                                         scale=1.0 / (H_SCALE * F_SCALE)).then_inc(s_yz_hi, 1)
                if more:
                    copy_tT(n, 0)
                    copy_tT(n, 1)
                    place_low_h(n)
                norm1(t, 0)
                norm1(t, 1)
                norm1(t, 2)
                if more:
                    copy_adjT(n)
                    copy_tT(n, 2)
                    copy_drow(n)

                def copy_agg(k):
                    act.wait_ge(agg_full, t.count(6, k + 1))
                    nc.scalar.activation(yz_hi[:, k % C, 2 * (k // C):2 * (k // C) + 2], pair(J_AGG[k]),
                                         ACT.Copy).then_inc(s_agg_hi, 1)

                copy_agg(0)
                norm1(t, 3)
                copy_agg(1)
                copy_agg(2)
                if more:
                    copy_scores(n)
                for c in range(C):
                    act.wait_ge(h2T_full, t.count(3, c + 1))
                    nc.scalar.activation(hT_hi[:, c], ps(J_H2T + c), ACT.Copy).then_inc(s_h2T_hi, 1)
                for k in range(C, 2 * C):
                    copy_agg(k)
                if more2:
                    norm0(t.plus(2))
                if more:
                    exp_scores(n)
                if more2:
                    high_h(t.plus(2), 0)
                if more:
                    exp_fusion(n)
                if more2:
                    high_h(t.plus(2), 1)
                if more:
                    copy_fT(n)
                    copy_af(n)
                if more2:
                    copy_hT(t.plus(2))

            def copy_weight(name, chunks=range(C)):
                for c in chunks:
                    act.wait_ge(prep_full, FULL[name] + c)
                    nc.scalar.activation(w_hi[name][:, c], prep_bank(name, c), ACT.Copy).then_inc(prep_hi, 1)

            first = Turn(0, 0)
            copy_weight("G")
            norm0(first)
            copy_hT(first)
            high_h(first, 0)
            high_h(first, 1)
            act.wait_ge(prep_dve, 4)
            for c in range(C):
                copy_tT(first, c)
            copy_adjT(first)
            copy_scores(first)
            copy_drow(first)
            copy_weight("W34T", (0,))
            exp_scores(first)
            copy_weight("W34T", (1,))
            exp_fusion(first)
            copy_weight("W34T", (2,))
            copy_weight("W3T")
            copy_weight("WadjT")
            norm0(Turn(0, 1))
            copy_weight("WrevT")
            high_h(Turn(0, 1), 0)
            copy_fT(first)
            copy_weight("WselfT")
            high_h(Turn(0, 1), 1)
            copy_af(first)
            copy_hT(Turn(0, 1))
            turns(act, turn, turn)

        @block.vector
        def _(dve):
            def norm0_stats(t):
                dve.wait_ge(x_in[t.par], t.dma(1, 1))
                for i in range(TILES):
                    nc.vector.bn_stats(st6[:, 0, i], xin[:, t.par, i]).then_inc(v_st0, 1)
                dve.wait_ge(v_st0, t.count(4, 4))
                nc.vector.memset(spacer[:], 0.0)
                for i in range(TILES):
                    nc.vector.bn_aggr(mv[:, 0, i], st6[:, 0, i]).then_inc(v_mv0, 1)
                dve.wait_ge(v_mv0, t.count(4, 4))
                wait(dve, g_rstd0, t.count(1, 0))
                nc.vector.tensor_scalar(ve[:, 0], mv[:, 0, :, 1], EPS, H_SCALE ** -2, ALU.add,
                                        ALU.mult).then_inc(v_ve0, 1)

            def norm0_shift(t):
                dve.wait_ge(g_rstd0, t.count(1, 1))
                wait(dve, s_h, t.count(4, 0))
                nc.vector.scalar_tensor_tensor(out=nmr[:, 0], in0=mv[:, 0, :, 0], scalar=-1.0, in1=rstd[:, 0],
                                               op0=ALU.mult, op1=ALU.mult).then_inc(v_nmr0, 1)

            def split_hT(t, c):
                dve.wait_ge(s_hT_hi, t.count(3, c + 1))
                nc.vector.tensor_tensor(hT_lo[:, c], ps(J_HT + c), hT_hi[:, c].bitcast(F32),
                                        ALU.subtract).then_inc(v_hT_lo, 1)

            def masks(t):
                adj_f = mask[:, 0:TILES]
                dve.wait_ge(adj_in[t.par], t.dma(1, 1))
                nc.vector.tensor_copy(adj_f, adj_i[:, t.par]).then_inc(v_adj, 1)
                dve.wait_ge(v_adj, t.count(10, 1))
                nc.vector.tensor_copy(adj_b[:, t.par, :, 0:P].rearrange("p t (h j) -> p t h j", h=2),
                                      adj_f.unsqueeze(2).broadcast_to([P, TILES, 2, N])).then_inc(v_adj, 1)
                for g in range(2):
                    for to in range(2):
                        nc.vector.tensor_copy(adj_b[graph(to), t.par, :, P + g * N:P + (g + 1) * N],
                                              mask[graph(g), 0:TILES]).then_inc(v_adj, 1)
                nc.vector.tensor_scalar(mask[:, TILES:], adj_f, -1.0, 1.0, ALU.mult, ALU.add).then_inc(v_adj, 1)
                nc.vector.tensor_scalar(neg[:, 0:TILES], adj_f, -1.0, BIG, ALU.add, ALU.mult).then_inc(v_adj, 1)
                nc.vector.tensor_scalar(neg[:, TILES:], adj_f, -BIG, None, ALU.mult).then_inc(v_adj, 1)
                nc.vector.tensor_reduce(deg[:, 0], adj_f, AX.X, ALU.add).then_inc(v_adj, 1)

            def degrees(t):
                def done(k):
                    dve.wait_ge(v_dcol, t.count(11, k))

                adjT = bank[J_ADJT % 8][:].bitcast(F16)[:, 0:W].rearrange("p (t h i) -> p t h i", t=TILES, h=2)
                dve.wait_ge(adjT_full, t.count(1, 1))
                dve.wait_ge(v_adj, t.count(10, 10))
                for g in range(2):
                    last = nc.vector.tensor_reduce(deg[graph(g), 1], adjT[graph(g), :, g], AX.X, ALU.add)
                last.then_inc(v_dcol, 1)
                done(1)
                nc.vector.tensor_scalar(ind[:], deg[:], 1.0, None, ALU.min).then_inc(v_dcol, 1)
                nc.vector.tensor_scalar(degc[:], deg[:], 1.0, None, ALU.max).then_inc(v_dcol, 1)
                done(3)
                nc.vector.tensor_scalar(noedge[:], ind[:, 0], -1.0, 1.0, ALU.mult, ALU.add).then_inc(v_dcol, 1)
                nc.vector.reciprocal(rdeg[:], degc[:]).then_inc(v_dcol, 1)
                for half in range(2):
                    nc.vector.tensor_copy(dcol[:, :, half, 0:2],
                                          deg[:].rearrange("p k t -> p t k")).then_inc(v_dcol, 1)
                    nc.vector.tensor_copy(dcol[:, :, half, 2:4],
                                          ind[:].rearrange("p k t -> p t k")).then_inc(v_dcol, 1)

            def edge_rows(t):
                dve.wait_ge(v_dcol, t.count(11, 9))
                nc.vector.tensor_scalar(rdeg_h[:, t.par], rdeg[:], 1.0 / H_SCALE, None, ALU.mult).then_inc(v_dcol, 1)
                nc.vector.tensor_tensor(edges[:], mask[:, 0:TILES],
                                        noedge[:].unsqueeze(2).broadcast_to([P, TILES, N]),
                                        ALU.add).then_inc(v_dcol, 1)

            def residual0(t, i):
                dve.wait_ge(x1_full, t.count(4, i + 1))
                dve.wait_ge(g_xb, t.count(4, i + 1))
                nc.vector.tensor_tensor(x1[:, t.par, i], ps(J_X1[i], D),
                                        x1[:, t.par, i], ALU.add).then_inc(v_x1, 1)
                dve.wait_ge(v_x1, t.count(4, i + 1))
                nc.vector.bn_stats(st6[:, 1, i], x1[:, t.par, i]).then_inc(v_st, 1)
                dve.wait_ge(v_st, t.count(4, i + 1))
                nc.vector.memset(spacer[:], 0.0)
                nc.vector.bn_aggr(mv[:, 1, i], st6[:, 1, i]).then_inc(v_mv, 1)
                dve.wait_ge(v_mv, t.count(4, i + 1))
                nc.vector.tensor_scalar(ve[:, 1, i:i + 1], mv[:, 1, i, 1:2], EPS, H_SCALE ** -2, ALU.add,
                                        ALU.mult).then_inc(v_ve, 1)

            def norm1_shift(t, i):
                dve.wait_ge(g_rstd, t.count(4, i + 1))
                nc.vector.scalar_tensor_tensor(out=nmr[:, 1, i:i + 1], in0=mv[:, 1, i, 0:1], scalar=-1.0,
                                               in1=rstd[:, 1, i:i + 1], op0=ALU.mult, op1=ALU.mult).then_inc(v_nmr, 1)

            def split_h2(t, i, graphs=range(2)):
                for g in graphs:
                    dve.wait_ge(s_h2_hi, t.count(8, 2 * i + g + 1))
                    nc.vector.tensor_tensor(h2_parts[graph(1 - g), i, g], h[graph(g), i], h2_parts[graph(g), i, g],
                                            ALU.subtract).then_inc(v_h2_lo, 1)

            def shift_scores(t):
                dve.wait_ge(s_sc, t.count(1, 1))
                nc.vector.tensor_tensor(a[:].rearrange("p (m t) j -> p m t j", m=2),
                                        sc[:].unsqueeze(1).broadcast_to([P, 2, TILES, N]),
                                        mask[:].rearrange("p (m t) j -> p m t j", m=2), ALU.mult).then_inc(v_a, 1)
                dve.wait_ge(v_a, t.count(3, 1))
                nc.vector.tensor_tensor(a[:], a[:], neg[:], ALU.add).then_inc(v_a, 1)
                dve.wait_ge(v_a, t.count(3, 2))
                nc.vector.tensor_reduce(amax[:], a[:], AX.X, ALU.max).then_inc(v_f, 1)
                dve.wait_ge(v_f, t.count(8, 1))
                nc.vector.tensor_tensor(a[:], a[:], amax[:].unsqueeze(2).broadcast_to([P, 2 * TILES, N]),
                                        ALU.subtract).then_inc(v_a, 1)

            def weights(t):
                dve.wait_ge(s_exp, t.count(1, 1))
                nc.vector.tensor_reduce(esum[:], e[:], AX.X, ALU.add).then_inc(v_f, 1)
                dve.wait_ge(v_f, t.count(8, 2))
                nc.vector.reciprocal(rsum[:], esum[:]).then_inc(v_f, 1)
                dve.wait_ge(v_f, t.count(8, 3))
                nc.vector.tensor_tensor(rsd[:], rsum[:, 0:TILES], rdeg[:, 0], ALU.mult).then_inc(v_f, 1)
                dve.wait_ge(v_f, t.count(8, 4))
                nc.vector.tensor_tensor(z[:], e[:, 0:TILES], rsd[:].unsqueeze(2).broadcast_to([P, TILES, N]),
                                        ALU.mult).then_inc(v_f, 1)

            def off_edge_weights(t):
                for g in range(2):
                    r = slice(g * N, (g + 1) * N)
                    last = nc.vector.tensor_tensor(An[r, :, r], e[r, TILES:],
                                                   rsum[r, TILES:].unsqueeze(2).broadcast_to([N, TILES, N]),
                                                   ALU.mult)
                last.then_inc(v_An, 1)

            def fusion(t):
                dve.wait_ge(s_zexp, t.count(1, 1))
                nc.vector.tensor_tensor(zm[:], zx[:], edges[:], ALU.mult).then_inc(v_f, 1)
                dve.wait_ge(v_f, t.count(8, 6))
                nc.vector.tensor_reduce(fsum[:], zm[:], AX.X, ALU.add).then_inc(v_f, 1)
                dve.wait_ge(v_f, t.count(8, 7))
                nc.vector.reciprocal(frec[:], fsum[:]).then_inc(v_f, 1)
                dve.wait_ge(v_f, t.count(8, 8))
                for half in range(2):
                    last = nc.vector.tensor_tensor(Fn[:, :, half * N:(half + 1) * N], zm[:],
                                                   frec[:].unsqueeze(2).broadcast_to([P, TILES, N]), ALU.mult)
                last.then_inc(v_Fn, 1)

            def split_fa(t, job, hi_ready, part, signal):
                dve.wait_ge(hi_ready, t.count(1, 1))
                nc.vector.scalar_tensor_tensor(out=fa_lo[:, :, part], in0=ps(job).rearrange("p (t i) -> p t i", t=TILES),
                                               scalar=F_SCALE, in1=fa_hi[:, :, part], op0=ALU.mult,
                                               op1=ALU.subtract).then_inc(signal, 1)

            def result(t, i):
                result_self(t, i)
                result_adj(t, i)
                result_rev(t, i)

            def result_self(t, i):
                y = x1[:, t.par, i]
                dve.wait_ge(out_full, t.count(12, N_SELF[i]))
                nc.vector.scalar_tensor_tensor(out=y, in0=ps(J_SELF[i], D), scalar=1.0 / H_SCALE, in1=y,
                                               op0=ALU.mult, op1=ALU.add).then_inc(v_out_step, 1)

            def result_adj(t, i):
                y = x1[:, t.par, i]
                dve.wait_ge(out_full, t.count(12, N_ADJ[i]))
                dve.wait_ge(v_out_step, t.count(8, 2 * i + 1))
                nc.vector.scalar_tensor_tensor(out=y, in0=ps(J_ADJ[i], D), scalar=rdeg_h[:, t.par, 0, i:i + 1], in1=y,
                                               op0=ALU.mult, op1=ALU.add).then_inc(v_out_step, 1)

            def result_rev(t, i):
                y = x1[:, t.par, i]
                dve.wait_ge(out_full, t.count(12, N_REV[i]))
                dve.wait_ge(v_out_step, t.count(8, 2 * i + 2))
                nc.vector.scalar_tensor_tensor(out=y, in0=ps(J_REV[i], D), scalar=rdeg_h[:, t.par, 1, i:i + 1], in1=y,
                                               op0=ALU.mult, op1=ALU.add).then_inc(v_out, 1)

            def split_yz(t, k):
                dve.wait_ge(s_yz_hi, t.count(6, k + 1))
                part = slice(2 * (k // C), 2 * (k // C) + 2)
                nc.vector.scalar_tensor_tensor(out=yz_lo[:, k % C, part],
                                               in0=bank[(J_YZ + k) % 8][:].rearrange("p (t i) -> p t i", t=2),
                                               scalar=1.0 / (H_SCALE * F_SCALE), in1=yz_hi[:, k % C, part].bitcast(F32),
                                               op0=ALU.mult, op1=ALU.subtract).then_inc(v_yz_lo, 1)

            def split_agg(t, k):
                dve.wait_ge(s_agg_hi, t.count(6, k + 1))
                part = slice(2 * (k // C), 2 * (k // C) + 2)
                nc.vector.tensor_tensor(yz_lo[:, k % C, part], bank[J_AGG[k] % 8][:].rearrange("p (t i) -> p t i", t=2),
                                        yz_hi[:, k % C, part].bitcast(F32), ALU.subtract).then_inc(v_agg_lo, 1)

            def split_h2T(t, c):
                dve.wait_ge(s_h2T_hi, t.count(3, c + 1))
                nc.vector.tensor_tensor(hT_lo[:, c], ps(J_H2T + c), hT_hi[:, c].bitcast(F32),
                                        ALU.subtract).then_inc(v_h2T_lo, 1)

            def turn(t):
                n, m = t.plus(1), t.plus(2)
                more, more2 = not is_last(t, 1), not is_last(t, 2)
                for k in range(2 * C):
                    split_yz(t, k)
                if more:
                    masks(n)
                if more2:
                    norm0_stats(m)
                residual0(t, 0)
                norm1_shift(t, 0)
                residual0(t, 1)
                split_h2(t, 0, (0,))
                norm1_shift(t, 1)
                split_h2(t, 0, (1,))
                residual0(t, 2)
                split_h2(t, 1, (0,))
                norm1_shift(t, 2)
                split_h2(t, 1, (1,))
                if more:
                    degrees(n)
                residual0(t, 3)
                split_h2(t, 2, (0,))
                norm1_shift(t, 3)
                split_h2(t, 2, (1,))
                split_agg(t, 0)
                split_h2(t, 3)
                split_agg(t, 1)
                split_agg(t, 2)
                for c in range(C):
                    split_h2T(t, c)
                if more2:
                    norm0_shift(m)
                for k in range(C, 2 * C):
                    split_agg(t, k)
                if more:
                    shift_scores(n)
                    edge_rows(n)
                result_self(t, 0)
                if more:
                    weights(n)
                result_adj(t, 0)
                if more:
                    off_edge_weights(n)
                result_rev(t, 0)
                if more:
                    fusion(n)
                result(t, 1)
                result(t, 2)
                if more:
                    split_fa(n, J_FT, s_fT_hi, slice(0, P), v_fT_lo)
                result_self(t, 3)
                result_adj(t, 3)
                if more:
                    split_fa(n, J_AT, s_af_hi, slice(P, 2 * P), v_af_lo)
                if more2:
                    split_hT(m, 0)
                result_rev(t, 3)
                if more2:
                    split_hT(m, 1)
                    split_hT(m, 2)

            def split_weight(name, chunks=range(C)):
                for c in chunks:
                    dve.wait_ge(prep_hi, names.index(name) * C + c + 1)
                    nc.vector.tensor_tensor(w_lo[name][:, c], prep_bank(name, c), w_hi[name][:, c].bitcast(F32),
                                            ALU.subtract).then_inc(prep_lo, 1)

            first = Turn(0, 0)
            norm0_stats(first)
            norm0_shift(first)
            split_weight("G")
            for c in range(C):
                dve.wait_ge(prep_full, FULL["W4T"] + c)
                nc.vector.tensor_copy(W4T[:, c], prep_bank("W4T", c)).then_inc(prep_dve, 1)
            dve.wait_ge(prep_full, FULL["b1W2"])
            nc.vector.tensor_scalar(tb[:], prep_bank("b1W2", n=C), H_SCALE, None, ALU.mult).then_inc(prep_dve, 1)
            for c in range(C):
                split_hT(first, c)
            masks(first)
            dve.wait_ge(c_in, 16 * 6)
            dve.wait_ge(consts_ready, 6)
            nc.vector.tensor_copy(b3m[:], b3c[:].unsqueeze(2).broadcast_to([P, C, P])).then_inc(prep_dve, 1)
            for k in range(2):
                nc.vector.tensor_copy(relL[:, k, k:k + LO + 1:LO],
                                      relE[:, k:k + 1].broadcast_to([P, 2])).then_inc(prep_dve, 1)
            nc.vector.tensor_tensor(bias0[:], bias0[:], b4bc[:], ALU.add).then_inc(prep_dve, 1)
            for g in range(2):
                dve.wait_ge(s_h_hi, g + 1)
                nc.vector.tensor_tensor(h_parts[graph(1 - g), 0, :, g], h[graph(g)], h_parts[graph(g), 0, :, g],
                                        ALU.subtract).then_inc(h_lo_placed, 1)
            degrees(first)
            norm0_stats(Turn(0, 1))
            dve.wait_ge(prep_full, FULL["bias"])
            dve.wait_ge(prep_dve, 8)
            nc.vector.tensor_tensor(bias0[:], prep_bank("bias"), bias0[:], ALU.add).then_inc(prep_dve, 1)
            shift_scores(first)
            norm0_shift(Turn(0, 1))
            edge_rows(first)
            split_weight("W34T", (0,))
            weights(first)
            off_edge_weights(first)
            split_weight("W34T", (1, 2))
            split_weight("W3T")
            for k, w in enumerate(("WrT", "WrrT")):
                dve.wait_ge(prep_full, FULL[w])
                nc.vector.tensor_copy(WrTs[:, k], prep_bank(w)).then_inc(prep_dve, 1)
            fusion(first)
            split_weight("WadjT")
            dve.wait_ge(r_in, 16 * 12)
            dve.wait_ge(prep_full, FULL["rows"])
            nc.vector.tensor_tensor(rows[:], prep_bank("rows")[0:64], rows_b[:], ALU.add).then_inc(prep_dve, 1)
            split_weight("WrevT")
            split_fa(first, J_FT, s_fT_hi, slice(0, P), v_fT_lo)
            split_weight("WselfT")
            split_fa(first, J_AT, s_af_hi, slice(P, 2 * P), v_af_lo)
            for c in range(C):
                split_hT(Turn(0, 1), c)
            dve.wait_ge(prep_dve, 12)
            nc.vector.tensor_scalar(rows[:], rows[:], H_SCALE, None, ALU.mult).then_inc(prep_dve, 1)
            dve.wait_ge(prep_dve, 13)
            nc.vector.tensor_copy(rows_r[:], rows[:]).then_inc(prep_dve, 1)
            nc.vector.tensor_copy(rank[0:LO], rows[0:LO]).then_inc(prep_dve, 1)
            dve.wait_ge(prep_dve, 14)
            nc.vector.tensor_tensor(rank[LO:64], rows[LO:64], rows_r[LO:64].bitcast(F32),
                                    ALU.subtract).then_inc(prep_dve, 1)
            turns(dve, turn, turn)

        @block.tensor
        def _(pe):
            def chunk(c):
                return slice(c * P, (c + 1) * P)

            def group(to, products):
                for k, (lhsT, rhs) in enumerate(products):
                    last = nc.tensor.matmul(to, lhsT, rhs, start=(k == 0), stop=(k == len(products) - 1))
                return last

            def three(l_hi, l_lo, r_hi, r_lo):
                return [(l_hi, r_hi), (l_hi, r_lo), (l_lo, r_hi)]

            def hT_job(t):
                pe.wait_ge(s_h, t.count(4, 4))
                for c in range(C):
                    for i in range(TILES):
                        last = nc.tensor.transpose(ps(J_HT + c)[:, chunk(i)], h[:, i, chunk(c)], id32[:])
                    last.then_inc(hT_full, 1)

            def t_job(t, c):
                if c == 0:
                    pe.wait_ge(v_hT_lo, t.count(3, 3))
                g = [three(w_hi["G"][:, d, chunk(c)], w_lo["G"][:, d, chunk(c)], hT_hi[:, d], hT_lo[:, d])
                     for d in range(C)]
                group(ps(J_T[c]), sum(g, [])).then_inc(t_full, 1)

            def adjT_job(t):
                pe.wait_ge(v_adj, t.count(10, 2))
                to = bank[J_ADJT % 8][:].bitcast(F16)
                for i in range(TILES):
                    last = nc.tensor.transpose(to[:, chunk(i)], adj_b[:, t.par, i, 0:P], id16[:])
                last.then_inc(adjT_full, 1)

            def drow_job(t):
                pe.wait_ge(v_dcol, t.count(11, 9))
                pe.wait_ge(s_adjT, t.count(1, 1))
                to = bank[J_ADJT % 8][:].bitcast(F16)
                for i in range(TILES):
                    last = nc.tensor.transpose(to[:, W + i * P:W + (i + 1) * P],
                                               dcol[:, i].rearrange("p a b -> p (a b)"), id16[:])
                last.then_inc(drow_full, 1)

            def att_job(t):
                pe.wait_ge(s_tT, t.count(3, 3))
                pe.wait_ge(g_hT, t.count(3, 3))
                for i in range(TILES):
                    last = group(ps(J_ATT)[:, chunk(i)], [(tT[:, c, chunk(i)], hT[:, c, chunk(i)]) for c in range(C)])
                last.then_inc(att_full, 1)

            def fT_job(t):
                pe.wait_ge(v_Fn, t.count(1, 1))
                for i in range(TILES):
                    last = nc.tensor.transpose(ps(J_FT)[:, chunk(i)], Fn[:, i], id32[:])
                last.then_inc(fT_full, 1)
                for i in range(TILES):
                    last = nc.tensor.transpose(ps(J_AT)[:, chunk(i)], An[:, i], id32[:])
                last.then_inc(aT_full, 1)

            def af_job(t):
                pe.wait_ge(s_AT, t.count(1, 1))
                for i in range(TILES):
                    last = group(ps(J_AT)[:, chunk(i)], [(Fn[:, i], AT[:, i])])
                last.then_inc(af_full, 1)

            def x1_job(t, i):
                y, zz = slice(0, P), slice(P, 2 * P)
                g = [three(yz_hi[:, c, i, part], yz_lo[:, c, i, part], w_hi[w][:, c], w_lo[w][:, c])
                     for w, part in (("W3T", y), ("W34T", zz)) for c in range(C)]
                group(ps(J_X1[i], D), sum(g, [])).then_inc(x1_full, 1)

            def self_job(t, i):
                g = [three(hT_hi[:, c, chunk(i)], hT_lo[:, c, chunk(i)], w_hi["WselfT"][:, c], w_lo["WselfT"][:, c])
                     for c in range(C)]
                group(ps(J_SELF[i], D), sum(g, [(drow[:, t.par, chunk(i)], rank[:])])).then_inc(out_full, 1)

            def neighbours_job(i, job, part, w):
                g = [three(yz_hi[:, c, i, part], yz_lo[:, c, i, part], w_hi[w][:, c], w_lo[w][:, c]) for c in range(C)]
                group(ps(job, D), sum(g, [])).then_inc(out_full, 1)

            def adj_job(i):
                neighbours_job(i, J_ADJ[i], slice(0, P), "WadjT")

            def rev_job(i):
                neighbours_job(i, J_REV[i], slice(P, 2 * P), "WrevT")

            def yz_job(t, k):
                for half in range(2):
                    i, c = 2 * (k // C) + half, k % C
                    to, hi, lo = (v.rearrange("p (m t) -> p m t", m=2) for v in (
                        ps(J_YZ + k)[:, half * 2 * P:(half + 1) * 2 * P], fa_hi[:, i], fa_lo[:, i]))
                    for g in range(2):
                        parts = h_parts[:, t.par, i, g, chunk(c)]
                        last = group(to[:, :, graph(g)], [(parts, hi[:, :, graph(g)]), (parts, lo[:, :, graph(g)])])
                last.then_inc(yz_full, 1)

            def agg_job(t, k):
                for half in range(2):
                    i, c = 2 * (k // C) + half, k % C
                    to, adjs = (v.rearrange("p (m t) -> p m t", m=2) for v in (
                        ps(J_AGG[k])[:, half * 2 * P:(half + 1) * 2 * P], adj_b[:, t.par, i]))
                    for g in range(2):
                        last = group(to[:, :, graph(g)], [(h2_parts[:, i, g, chunk(c)], adjs[:, :, graph(g)])])
                last.then_inc(agg_full, 1)

            def turn(t):
                n, m = t.plus(1), t.plus(2)
                more, more2 = not is_last(t, 1), not is_last(t, 2)
                pe.wait_ge(v_fT_lo, t.count(1, 1))
                pe.wait_ge(v_af_lo, t.count(1, 1))
                pe.wait_ge(h_lo_placed, t.count(2, 2))
                for k in range(2 * C):
                    if k == 2:
                        wait(pe, v_out, t.count(4, 0))
                    if k >= 4 and more:
                        pe.wait_ge(v_hT_lo, n.count(3, k - 3))
                    yz_job(t, k)
                if more:
                    t_job(n, 0)
                    t_job(n, 1)
                pe.wait_ge(v_yz_lo, t.count(6, 3))
                x1_job(t, 0)
                x1_job(t, 1)
                if more:
                    adjT_job(n)
                pe.wait_ge(v_yz_lo, t.count(6, 6))
                x1_job(t, 2)
                x1_job(t, 3)
                if more:
                    t_job(n, 2)
                    drow_job(n)
                pe.wait_ge(s_adjT, t.count(1, 1))
                pe.wait_ge(v_adj, t.count(10, 6))
                pe.wait_ge(v_h2_lo, t.count(8, 4))
                for k in range(C):
                    agg_job(t, k)
                if more:
                    att_job(n)
                if more:
                    pe.wait_ge(s_drow, n.count(1, 1))
                pe.wait_ge(v_x1, t.count(4, 3))
                for i in range(TILES):
                    pe.wait_ge(s_h2, t.count(4, i + 1))
                    for c in range(C):
                        last = nc.tensor.transpose(ps(J_H2T + c)[:, chunk(i)], h[:, i, chunk(c)], id32[:])
                        if i == TILES - 1:
                            last.then_inc(h2T_full, 1)
                pe.wait_ge(v_h2_lo, t.count(8, 8))
                for k in range(C, 2 * C):
                    if k == 4 and more:
                        pe.wait_ge(s_sc, n.count(1, 1))
                    if k == 5:
                        pe.wait_ge(v_agg_lo, t.count(6, 1))
                    agg_job(t, k)
                pe.wait_ge(v_agg_lo, t.count(6, 3))
                adj_job(0)
                rev_job(0)
                pe.wait_ge(s_drow, t.count(1, 1))
                pe.wait_ge(v_h2T_lo, t.count(3, 3))
                if isinstance(t.it, int) and t.index == 0:
                    pe.wait_ge(prep_dve, 16)
                self_job(t, 0)
                self_job(t, 1)
                adj_job(1)
                pe.wait_ge(v_agg_lo, t.count(6, 6))
                rev_job(1)
                self_job(t, 2)
                adj_job(2)
                pe.wait_ge(v_out, t.count(4, 1))
                rev_job(2)
                if more:
                    fT_job(n)
                pe.wait_ge(v_out, t.count(4, 2))
                self_job(t, 3)
                adj_job(3)
                if more:
                    af_job(n)
                pe.wait_ge(v_out, t.count(4, 3))
                if more2:
                    hT_job(m)
                rev_job(3)

            def transposed(name, natural_w):
                for c in range(C):
                    for o in range(C):
                        last = nc.tensor.transpose(prep_bank(name, c)[:, chunk(o)], natural_w[:, o, chunk(c)], id32[:])
                    last.then_inc(prep_full, 1)

            def W34_job(c):
                group(prep_bank("W34T", c), [(W3n[:, o, chunk(c)], W4T[:, o]) for o in range(C)]).then_inc(prep_full, 1)

            first = Turn(0, 0)
            for o in range(C):
                pe.wait_ge(w12_in[o], 32)
                for c in range(C):
                    last = nc.tensor.matmul(prep_bank("G", c), W1n[:, o, chunk(c)], W2n[:, o],
                                            start=(o == 0), stop=(o == C - 1))
                    if o == C - 1:
                        last.then_inc(prep_full, 1)
            pe.wait_ge(ident_ready, 2)
            pe.wait_ge(w_in["W4"], 16)
            transposed("W4T", W4n)
            pe.wait_ge(c_in, 16 * 6)
            for c in range(C):
                last = group(prep_bank("b1W2", n=C)[:, c:c + 1],
                             [(W2n[:, o, chunk(c)], b1c[:, o:o + 1]) for o in range(C)])
            last.then_inc(prep_full, 1)
            pe.wait_ge(prep_dve, 4)
            hT_job(first)
            pe.wait_ge(prep_lo, 3)
            for c in range(C):
                t_job(first, c)
            adjT_job(first)
            pe.wait_ge(prep_dve, 5)
            group(prep_bank("bias"), [(b3m[:, o], W4T[:, o]) for o in range(C)]).then_inc(prep_full, 1)
            att_job(first)
            drow_job(first)
            pe.wait_ge(w_in["W3"], 16)
            for c in range(C):
                group(prep_bank("W34T", c), [(W3n[:, o, chunk(c)], W4T[:, o]) for o in range(C)]).then_inc(prep_full, 1)
            pe.wait_ge(s_drow, 1)
            pe.wait_ge(s_sc, 1)
            transposed("W3T", W3n)
            pe.wait_ge(r_in, 16 * 12)
            pe.wait_ge(prep_dve, 9)
            for k, w in enumerate(("WrT", "WrrT")):
                for o in range(C):
                    last = nc.tensor.transpose(prep_bank(w)[:, chunk(o)], WrN[:, k, o], id32[:])
                last.then_inc(prep_full, 1)
            pe.wait_ge(w_in["Wadj"], 16)
            pe.wait_ge(prep_lo, 6)
            transposed("WadjT", W1n)
            pe.wait_ge(w_in["Wrev"], 16)
            pe.wait_ge(prep_lo, 9)
            pe.wait_ge(prep_dve, 11)
            transposed("WrevT", W2n)
            group(prep_bank("rows")[0:64], [(relL[:, k], WrTs[:, k]) for k in range(2)]).then_inc(prep_full, 1)
            pe.wait_ge(prep_lo, 12)
            fT_job(first)
            pe.wait_ge(w_in["Wself"], 16)
            pe.wait_ge(prep_dve, 12)
            transposed("WselfT", W3n)
            af_job(first)
            pe.wait_ge(prep_lo, 18)
            hT_job(Turn(0, 1))
            turns(pe, turn, turn)


INPUTS = ("x", "adj", "L0_gnn_W1", "L0_gnn_b1", "L0_gnn_W2", "L0_gnn_b2", "L0_gnn_W3", "L0_gnn_b3", "L0_gnn_W4",
          "L0_gnn_b4", "L1_gnn_E", "L1_gnn_Wadj", "L1_gnn_badj", "L1_gnn_Wrev", "L1_gnn_brev", "L1_gnn_Wself",
          "L1_gnn_bself", "L1_gnn_Wr", "L1_gnn_br", "L1_gnn_Wrr", "L1_gnn_brr")


def kernel(**inputs):
    import numpy as np
    import concourse.bacc as bacc
    from concourse.bass_utils import run_bass_kernel_spmd

    nc = bacc.Bacc("TRN2", target_bir_lowering=False, num_devices=1)
    arrays, d = {}, {}
    for name in INPUTS:
        v = np.ascontiguousarray(inputs[name])
        arrays[f"in_{name}"] = v
        d[name] = nc.dram_tensor(f"in_{name}", v.shape, mybir.dt.from_np(v.dtype), kind="ExternalInput").ap()
    out = nc.dram_tensor("out", (GRAPHS, N, D), F32, kind="ExternalOutput").ap()
    a, b = "L0_gnn_", "L1_gnn_"
    build(nc, d["x"], d["adj"], [d[a + w] for w in ("W1", "W2", "W3", "W4")],
          [d[a + w] for w in ("b1", "b2", "b3", "b4")], d[b + "E"],
          [d[b + w] for w in ("Wadj", "Wrev", "Wself")], [d[b + w] for w in ("badj", "brev", "bself")],
          d[b + "Wr"], d[b + "br"], d[b + "Wrr"], d[b + "brr"], out)
    r = run_bass_kernel_spmd(nc, [arrays], core_ids=[0])
    return r.results[0]["out"]
```
